# Optimizing a Trainium2 kernel written in Bass

```python
import numpy as np
import jax
import jax.numpy as jnp

def _softmax(x, axis=-1):
    return jax.nn.softmax(x, axis=axis)

def _gelu(x):
    return jax.nn.gelu(x, approximate=True)

def _silu(x):
    return jax.nn.silu(x)

def _sigmoid(x):
    return jax.nn.sigmoid(x)

def _layernorm(x, axis=-1, eps=1e-05):
    m = jnp.mean(x, axis=axis, keepdims=True)
    v = jnp.var(x, axis=axis, keepdims=True)
    return (x - m) / jnp.sqrt(v + eps)

def _scatter_add(tgt, idx, src, axis=0):
    return tgt.at[idx].add(src)

def _segment_sum(src, seg, n):
    return jax.ops.segment_sum(src, seg, n)
kernel_name = 'mk_rec_standalone_d1_rec_r8_4ff927'

def setup_inputs(seed: int=0):
    np.random.seed(seed)
    _w = jnp.asarray

    def _rec_inputs():
        import jax
        import jax.numpy as jnp
        _rk = jax.random.key(seed)
        r_feature_emb = -0.000611745 + 1.00059 * jax.random.normal(jax.random.fold_in(_rk, 1), (512, 39, 64), jnp.float32)
        return r_feature_emb
    r_feature_emb = _rec_inputs()

    def _L0_rec_setup():
        import jax, jax.numpy as jnp
        import numpy as np
        B, F, D = (1024, 39, 64)
        UNITS = [64, 64, 64]
        key = jax.random.key(seed)
        ks = jax.random.split(key, 16)
        inp = {'feature_emb': jax.random.normal(ks[0], (B, F, D), dtype=jnp.float32)}
        for i in range(3):
            inp[f'gw{i + 1}'] = jax.random.normal(ks[1 + i], (D, D), dtype=jnp.float32) * (1.0 / np.sqrt(D))
            inp[f'gb{i + 1}'] = jnp.zeros((D,), dtype=jnp.float32)
        m_prev = F
        for i, u in enumerate(UNITS):
            fan_in = F * m_prev
            inp[f'cw{i + 1}'] = jax.random.normal(ks[5 + i], (u, F, m_prev), dtype=jnp.float32) * (1.0 / np.sqrt(fan_in))
            inp[f'cb{i + 1}'] = jnp.zeros((u,), dtype=jnp.float32)
            m_prev = u
        inp['fcW'] = jax.random.normal(ks[9], (1, sum(UNITS)), dtype=jnp.float32) * (1.0 / np.sqrt(sum(UNITS)))
        inp['fcb'] = jnp.zeros((1,), dtype=jnp.float32)
        return inp
    _L0_rec_all = _L0_rec_setup()
    _L0_rec_in = {k: v for k, v in _L0_rec_all.items() if k in ('gw1', 'gb1', 'gw2', 'gb2', 'gw3', 'gb3', 'cw1', 'cb1', 'cw2', 'cb2', 'cw3', 'cb3', 'fcW', 'fcb')}
    del _L0_rec_all
    return {'r_feature_emb': r_feature_emb, 'L0_rec_gw1': _L0_rec_in['gw1'], 'L0_rec_gb1': _L0_rec_in['gb1'], 'L0_rec_gw2': _L0_rec_in['gw2'], 'L0_rec_gb2': _L0_rec_in['gb2'], 'L0_rec_gw3': _L0_rec_in['gw3'], 'L0_rec_gb3': _L0_rec_in['gb3'], 'L0_rec_cw1': _L0_rec_in['cw1'], 'L0_rec_cb1': _L0_rec_in['cb1'], 'L0_rec_cw2': _L0_rec_in['cw2'], 'L0_rec_cb2': _L0_rec_in['cb2'], 'L0_rec_cw3': _L0_rec_in['cw3'], 'L0_rec_cb3': _L0_rec_in['cb3'], 'L0_rec_fcW': _L0_rec_in['fcW'], 'L0_rec_fcb': _L0_rec_in['fcb']}

def reference(r_feature_emb, L0_rec_gw1, L0_rec_gb1, L0_rec_gw2, L0_rec_gb2, L0_rec_gw3, L0_rec_gb3, L0_rec_cw1, L0_rec_cb1, L0_rec_cw2, L0_rec_cb2, L0_rec_cw3, L0_rec_cb3, L0_rec_fcW, L0_rec_fcb):
    import jax
    import jax.numpy as jnp

    def _L0_rec_ref(feature_emb, gw1, gb1, gw2, gb2, gw3, gb3, cw1, cb1, cw2, cb2, cw3, cb3, fcW, fcb):
        import jax, jax.numpy as jnp
        import numpy as np
        B, F, D = (1024, 39, 64)
        UNITS = [64, 64, 64]
        X0 = feature_emb
        X = X0
        layers = [(gw1, gb1, cw1, cb1), (gw2, gb2, cw2, cb2), (gw3, gb3, cw3, cb3)]
        pools = []
        for gw, gb, cw, cb in layers:
            H = jnp.einsum('bhd,de->bhe', X0, gw) + gb
            Xn = jnp.einsum('bhd,bmd,ohm->bod', H, X, cw) + cb[None, :, None]
            pools.append(Xn.sum(axis=-1))
            X = Xn
        rep = jnp.concatenate(pools, axis=-1)
        return rep @ fcW.T + fcb
    y = _L0_rec_ref(r_feature_emb, L0_rec_gw1, L0_rec_gb1, L0_rec_gw2, L0_rec_gb2, L0_rec_gw3, L0_rec_gb3, L0_rec_cw1, L0_rec_cb1, L0_rec_cw2, L0_rec_cb2, L0_rec_cw3, L0_rec_cb3, L0_rec_fcW, L0_rec_fcb)
    return y

_drawn_inputs = setup_inputs


def setup_inputs(seed=0):
    import zlib

    import numpy as np

    out = dict(_drawn_inputs(seed))
    spreads = {'L0_rec_gb1': (0.0, 0.1),
     'L0_rec_gb2': (0.0, 0.1),
     'L0_rec_gb3': (0.0, 0.1),
     'L0_rec_cb1': (0.0, 0.1),
     'L0_rec_cb2': (0.0, 0.1),
     'L0_rec_cb3': (0.0, 0.1)}
    factors = {}
    for name, (base, spread) in spreads.items():
        noise = np.random.default_rng([zlib.crc32(name.encode()), seed]).standard_normal(out[name].shape)
        drawn = base * np.exp(spread * noise) if base else spread * noise
        out[name] = jnp.asarray(drawn.astype(out[name].dtype))
    for name, factor in factors.items():
        out[name] = (out[name] * factor).astype(out[name].dtype)
    return out
```

```python
from contextlib import ExitStack

import numpy as np

import concourse.bass as bass
from concourse import mybir

F32 = mybir.dt.float32
F32R = mybir.dt.float32r
ALU = mybir.AluOpType
ACT = mybir.ActivationFunctionType
AX_X = mybir.AxisListType.X

B, F, D = 512, 39, 64
O = 64
SIDE_B = 8
N = SIDE_B * D
PAIRS = B // (2 * SIDE_B)

U1, V1 = 6, 20
J1, I1 = -(-F // U1), -(-F // V1)
V1_STARTS = (0, F - V1)
U2, V2 = 8, 16
J2, I2 = -(-F // U2), O // V2
K1, K2 = U1 * V1, U2 * V2
REST = 64
KH = REST + F
POOL_TILES = 2

ORDER = [(1, 0), (1, 1), (2, 0), (1, 2), (1, 3), (2, 1), (1, 4), (1, 5), (2, 2), (1, 6), (2, 3), (2, 4)]
UNITS = len(ORDER)
T_X2 = 1
T_W3 = 7
T_G = 2
T_H = 4
T_X1 = 10
T_SPREAD = 11
QUARTERS = 4
QB = SIDE_B // QUARTERS
SPREADS = 2 * I2
BUFS = 3
assert UNITS % BUFS == 0 and UNITS % 2 == 0 and J1 + J2 == UNITS


class Step:

    def __init__(self, n, static, trip=0):
        self.n, self.static, self.trip = n, static, trip
        self.has1 = static < PAIRS
        self.has2 = static >= 1
        self.has_h = static + 1 < PAIRS
        self.slots = [t for t, (layer, _) in enumerate(ORDER) if (layer == 1 and self.has1) or (layer == 2 and self.has2)]
        self.before = 0 if static == 0 else (n - 1) * UNITS + J1
        self.before_static = 0 if static == 0 else (static - 1) * UNITS + J1

    def unit(self, t):
        k = self.slots.index(t)
        return (*ORDER[t], self.before + k, self.before_static + k)


def ahead(step, following, t):
    k = step.slots.index(t) + 2
    if k < len(step.slots):
        return step, step.unit(step.slots[k])
    if following is None:
        return None, None
    return following, following.unit(following.slots[k - len(step.slots)])


def steps_of(eng, run, last=PAIRS):
    first = 2
    for n in range(first):
        run(Step(n, n), Step(n + 1, n + 1))
    trips = (PAIRS - 1 - first) // BUFS
    with eng.Fori(0, trips) as trip:
        for k in range(BUFS):
            n = first + k
            run(Step(trip * BUFS + n, n, trip), Step(trip * BUFS + n + 1, n + 1, trip))
    for n in range(first + trips * BUFS, last + 1):
        run(Step(n, n), Step(n + 1, n + 1) if n < last else None)


def wait(eng, sem, value):
    if not isinstance(value, int) or value > 0:
        eng.wait_ge(sem, value)


def cin_kernel(nc, x0t, x0h, gw, c1_in, c2_in, cw3, fc3, cols, rows, sel_in, out):
    with ExitStack() as ctx:
        def sb(name, shape, dt=F32):
            return ctx.enter_context(nc.sbuf_tensor(name, shape, dt))

        def sem(name):
            return ctx.enter_context(nc.semaphore(name))

        x0t_sb = sb("x0t_sb", [D + 1, BUFS, 2 * SIDE_B * F])
        x0rep = sb("x0rep", [K1, BUFS, I1, 2 * N])
        gw_sb = sb("gw_sb", [D + 1, 3 * D])
        c1 = sb("c1", [K1, J1, I1, O])
        c2 = sb("c2", [K2, J2, I2, O])
        w3 = sb("w3", [KH, 2 * O])
        fc3_sb = sb("fc3_sb", [KH, O])
        cols_sb = sb("cols_sb", [128, 7])
        rows_sb = sb("rows_sb", [2, 2 * O + 1])
        sel_raw = sb("sel_raw", [128, J1 * K1 + J2 * K2 + I2 * K2])
        sel = sb("sel", [128, J1 * K1 + J2 * K2 + I2 * K2], F32R)
        hsplit = sb("hsplit", [128, BUFS, 2, 2, N], F32R)
        h3 = sb("h3", [KH, BUFS, N])
        x1split = sb("x1split", [128, 2, N], F32R)
        x1rep = sb("x1rep", [K2, 2, I2, N])
        hpool = sb("hpool", [K2, 2, N])
        prod = sb("prod", [128, BUFS, 2, I2, N])
        g_sb = sb("g_sb", [128, N])
        x2g = sb("x2g", [128, N])
        x1sum = sb("x1sum", [128, PAIRS * SIDE_B])
        ysum = sb("ysum", [128, PAIRS * SIDE_B])
        x1tot = sb("x1tot", [128, PAIRS * SIDE_B])
        cb1d = sb("cb1d", [128, 1])
        const_row = sb("const_row", [2, O])
        const_y = sb("const_y", [2, 2])
        y_sb = sb("y_sb", [2, PAIRS * SIDE_B])

        ps = ctx.enter_context(nc.psum_tensor("ps", [128, 8, N], F32))
        acc1, acc2, misc = ps[:, 4, :], ps[:, 5, :], (ps[:, 6, :], ps[:, 7, :])

        cb1, cb2, fc2 = cols_sb[:, 0:1], cols_sb[:, 1:2], cols_sb[:, 2:3]
        fc1_sides, one_sides = cols_sb[:, 3:5], cols_sb[:, 5:7]
        sel1 = sel[:, 0:J1 * K1].rearrange("k (j p) -> k j p", j=J1)
        sel2 = sel[:, J1 * K1:J1 * K1 + J2 * K2].rearrange("k (j p) -> k j p", j=J2)
        sel_x = sel[:, J1 * K1 + J2 * K2:].rearrange("k (i p) -> k i p", i=I2)

        weights_in = sem("weights_in")
        constants_in = sem("constants_in")
        w3_in = sem("w3_in")
        x0t_in = [sem(f"x0t_in{k}") for k in range(BUFS)]
        x0rep_in = [sem(f"x0rep_in{k}") for k in range(BUFS)]
        zeros_done = sem("zeros_done")
        sel_done = sem("sel_done")
        w3_mult = sem("w3_mult")
        w3_done = sem("w3_done")
        h_made = sem("h_made")
        h_head = sem("h_head")
        h_rest = sem("h_rest")
        spread = sem("spread")
        hpool_copied = sem("hpool_copied")
        multiplied = sem("multiplied")
        pool_multiplied = sem("pool_multiplied")
        contracted = sem("contracted")
        x1_head = sem("x1_head")
        x1_rest = sem("x1_rest")
        x1_spread = sem("x1_spread")
        x1_copied = sem("x1_copied")
        g_made = sem("g_made")
        g_copied = sem("g_copied")
        x2_taken = sem("x2_taken")
        sums_done = sem("sums_done")
        prep = sem("prep")
        y_made = sem("y_made")
        y_done = sem("y_done")
        y_out = sem("y_out")

        def rep_bank(u, side):
            return ps[:, 2 * (u % 2) + side, :]

        def w3_stage():
            return x1rep[0:KH, :, :, :].rearrange("p s i n -> p (s i n)").rearrange("p (m o) -> p m o", o=O)

        block = ctx.enter_context(nc.Block())

        @block.sync
        def _(sp):
            def load_pair(m, buf, free_units):
                if free_units is not None:
                    sp.wait_ge(h_made, (m - BUFS + 1) * QUARTERS)
                sp.dma_start(x0t_sb[0:D, buf, :], x0t[:, bass.ds(m * (2 * SIDE_B * F), 2 * SIDE_B * F)]).then_inc(x0t_in[buf], 16)
                if free_units is not None:
                    sp.wait_ge(multiplied, 2 * free_units)
                for i, v0 in enumerate(V1_STARTS):
                    for u in range(U1):
                        sp.dma_start(x0rep[u * V1:(u + 1) * V1, buf, i, :],
                                     x0h[v0:v0 + V1, bass.ds(m * (2 * N), 2 * N)]).then_inc(x0rep_in[buf], 16)

            def layer1_end(n):
                return J1 if isinstance(n, int) and n == 0 else (n - 1) * UNITS + J1 + ORDER.index((1, J1 - 1)) + 1

            sp.dma_start(gw_sb[:, :], gw[:, :]).then_inc(weights_in, 16)
            sp.dma_start(sel_raw[:, :], sel_in[:, :]).then_inc(weights_in, 16)
            load_pair(0, 0, None)
            sp.dma_start(c1[:, :, :, :].rearrange("p j i o -> p (j i o)"), c1_in[:, :]).then_inc(constants_in, 16)
            sp.dma_start(cols_sb[:, :], cols[:, :]).then_inc(constants_in, 16)
            sp.dma_start(c2[:, :, :, :].rearrange("p j i o -> p (j i o)"), c2_in[:, :]).then_inc(constants_in, 16)
            sp.dma_start(rows_sb[:, :], rows[:, :]).then_inc(constants_in, 16)
            cw3_to = x1rep[:, :, :, :].rearrange("p s i n -> p (s i n)")
            sp.dma_start(cw3_to[0:F, :], cw3[:, :]).then_inc(w3_in, 16)
            sp.dma_start(cw3_to[F:REST, :], cw3[0:REST - F, :]).then_inc(w3_in, 16)
            sp.dma_start(cw3_to[REST:KH, :], cw3[:, :]).then_inc(w3_in, 16)
            sp.dma_start(fc3_sb[:, :], fc3[:, :].to_broadcast([KH, O])).then_inc(w3_in, 16)
            load_pair(1, 1, None)
            load_pair(2, 2, None)
            load_pair(3, 0, layer1_end(0))
            trips = (PAIRS - 4) // BUFS
            with sp.Fori(0, trips) as trip:
                for k in range(BUFS):
                    m = trip * BUFS + 4 + k
                    load_pair(m, (4 + k) % BUFS, layer1_end(m - BUFS))
            for m in range(4 + trips * BUFS, PAIRS):
                load_pair(m, m % BUFS, layer1_end(m - BUFS))
            sp.wait_ge(y_done, 1)
            sp.dma_start(out.rearrange("(n s b) o -> s n (b o)", s=2, b=SIDE_B),
                         y_sb[:, :].rearrange("s (n b) -> s n b", b=SIDE_B)).then_inc(y_out, 16)
            sp.wait_ge(y_out, 16)

        @block.tensor
        def _(pe):
            def make_h(q, buf, uses):
                if q == 0:
                    pe.wait_ge(x0t_in[buf], uses * 16)
                bank = misc[q % 2]
                for b in range(QB):
                    for side in range(2):
                        row = side * SIDE_B + q * QB + b
                        last = nc.tensor.matmul(bank[side * REST:side * REST + F, b * 3 * D:(b + 1) * 3 * D],
                                                x0t_sb[:, buf, row * F:(row + 1) * F], gw_sb[:, :], start=True, stop=True)
                last.then_inc(h_made, 1)

            def spread_h(step, unit):
                layer, j, u, us = unit
                pair_static = step.static if layer == 1 else step.static - 1
                for side in range(2):
                    wait(pe, multiplied, 2 * (u - 2) + side + 1)
                    lhs = sel1[0:KH, j, :] if layer == 1 else sel2[0:KH, j, :]
                    k = K1 if layer == 1 else K2
                    nc.tensor.matmul(rep_bank(us, side)[0:k, :], lhs, hsplit[0:KH, pair_static % BUFS, side, layer - 1, :],
                                     start=True, stop=True).then_inc(spread, 1)

            def spread_x1(k, n):
                side, i = divmod(k, I2)
                nc.tensor.matmul(misc[1 - k % 2][:, :], sel_x[:, i, :], x1split[:, side, :], start=True, stop=True).then_inc(x1_spread, 1)

            def before_spread_x1(k, step):
                n = step.n
                if k >= 2:
                    pe.wait_ge(x1_copied, n * SPREADS + k - 1)
                elif k == 1 and step.has2:
                    pe.wait_ge(g_copied, n)
                elif step.has_h:
                    pe.wait_ge(h_rest, (n + 1) * QUARTERS + (QUARTERS if k == 0 else QUARTERS - 1))
                else:
                    wait(pe, x1_copied, n * SPREADS - 1 + k)

            def contract(step, t, between):
                layer, j, u, us = step.unit(t)
                acc, c, tiles, k = (acc1, c1, I1, K1) if layer == 1 else (acc2, c2, I2, K2)
                units = J1 if layer == 1 else J2
                if j == 0:
                    if layer == 1:
                        wait(pe, x1_rest, step.n)
                    else:
                        wait(pe, x2_taken, step.n - 1)
                pe.wait_ge(multiplied, 2 * (u + 1))
                for i in range(tiles):
                    if layer == 2 and i == (0 if between else I2 - POOL_TILES):
                        pe.wait_ge(pool_multiplied, (step.n - 1) * J2 + j + 1)
                    for side in range(2):
                        last = nc.tensor.matmul(acc[side * O:(side + 1) * O, :], c[:, j, i, :], prod[0:k, us % BUFS, side, i, :],
                                                start=(j == 0 and i == 0), stop=(j == units - 1 and i == tiles - 1))
                    if i == tiles - 1:
                        last.then_inc(contracted, 1)
                    if between:
                        between(i)

            def run(step, following):
                n = step.n

                def spread_two(i):
                    if i == 0:
                        pe.wait_ge(x1_rest, n + 1)
                    for k in (2 * i, 2 * i + 1):
                        before_spread_x1(k, step)
                        spread_x1(k, n)

                def spread_ahead(t):
                    other, unit = ahead(step, following, t)
                    if unit is not None:
                        if unit[:2] == (1, 0):
                            pe.wait_ge(h_rest, (other.n + 1) * QUARTERS)
                        spread_h(other, unit)

                for t in range(UNITS):
                    present = t in step.slots
                    if present and step.static > 0:
                        spread_ahead(t)
                    if t == T_G and step.has2:
                        if step.static == 1:
                            pe.wait_ge(w3_done, 1)
                        pe.wait_ge(x1_copied, n * SPREADS)
                        nc.tensor.matmul(misc[0][:, :], w3[:, :], h3[0:KH, (step.static - 1) % BUFS, :],
                                         start=True, stop=True).then_inc(g_made, 1)
                    if T_H <= t < T_H + QUARTERS and step.has_h:
                        q = t - T_H
                        if q == 0:
                            wait(pe, g_copied, n)
                        elif q == 1:
                            wait(pe, x1_copied, n * SPREADS - 1)
                        else:
                            pe.wait_ge(h_rest, (n + 1) * QUARTERS + q - 1)
                        m = step.static + 1
                        make_h(q, m % BUFS, step.trip + m // BUFS + 1)
                    if present and step.static == 0:
                        spread_ahead(t)
                    if t == T_SPREAD and step.has1 and not present:
                        for i in range(I2):
                            spread_two(i)
                    elif present:
                        contract(step, t, spread_two if t == T_SPREAD and step.has1 else None)

            pe.wait_ge(weights_in, 32)
            pe.wait_ge(zeros_done, 4)
            for q in range(QUARTERS):
                if q >= 2:
                    pe.wait_ge(h_rest, q - 1)
                make_h(q, 0, 1)
            pe.wait_ge(sel_done, 1)
            pe.wait_ge(h_rest, QUARTERS)
            first = Step(0, 0)
            spread_h(first, first.unit(0))
            spread_h(first, first.unit(1))
            pe.wait_ge(constants_in, 64)
            steps_of(pe, run)
            pe.wait_ge(sums_done, 1)
            nc.tensor.matmul(misc[1][0:2, 0:PAIRS * SIDE_B], one_sides, ysum[:, :], start=True, stop=False)
            nc.tensor.matmul(misc[1][0:2, 0:PAIRS * SIDE_B], fc1_sides, x1tot[:, :], start=False, stop=True).then_inc(y_made, 1)

        @block.scalar
        def _(act):
            def heads(q, m, buf):
                act.wait_ge(h_made, m * QUARTERS + q + 1)
                cut = slice(q * QB * D, (q + 1) * QB * D)
                for side in range(2):
                    rows_ = slice(side * REST, side * REST + F)
                    src = misc[q % 2][rows_, 0:QB * 3 * D].rearrange("h (b l e) -> h b l e", b=QB, l=3)
                    dst = hsplit[rows_, buf, side, :, cut].rearrange("h l (b e) -> h b l e", b=QB)
                    nc.scalar.copy(dst, src[:, :, 0:2, :])
                    last = nc.scalar.copy(h3[rows_, buf, cut].rearrange("h (b e) -> h b e", b=QB), src[:, :, 2, :])
                last.then_inc(h_head, 1)

            def copy_for_pool(step, unit):
                layer, j, u, us = unit
                k = (step.n - 1) * J2 + j
                act.wait_ge(spread, 2 * (u + 1))
                wait(act, pool_multiplied, k if j == 0 else k - 1)
                nc.scalar.copy(hpool[:, j % 2, :], rep_bank(us, 1)).then_inc(hpool_copied, 1)

            def run(step, following):
                n = step.n
                for t in range(UNITS):
                    if t in step.slots:
                        other, unit = ahead(step, following, t)
                        if unit is not None and unit[0] == 2:
                            copy_for_pool(other, unit)
                    if t == T_G and step.has2:
                        act.wait_ge(g_made, n)
                        wait(act, x2_taken, n - 1)
                        nc.scalar.activation(g_sb[:, :], misc[0][:, :], ACT.Identity, bias=fc2).then_inc(g_copied, 1)
                    if T_H <= t < T_H + QUARTERS and step.has_h:
                        heads(t - T_H, n + 1, (step.static + 1) % BUFS)
                    if t == T_X1 - 1 and step.has1:
                        act.wait_ge(contracted, step.unit(9)[2] + 1)
                        for side in range(2):
                            half = slice(side * O, (side + 1) * O)
                            last = nc.scalar.activation(x1split[half, side, :], acc1[half, :], ACT.Identity, bias=cb1[half, :])
                        last.then_inc(x1_head, 1)
                    if t == T_SPREAD and step.has1:
                        if step.static == 0:
                            act.wait_ge(w3_done, 1)
                        for k in range(SPREADS):
                            side, i = divmod(k, I2)
                            act.wait_ge(x1_spread, n * SPREADS + k + 1)
                            nc.scalar.copy(x1rep[:, side, i, :], misc[1 - k % 2][:, :]).then_inc(x1_copied, 1)

            act.wait_ge(zeros_done, 4)
            for q in range(QUARTERS):
                heads(q, 0, 0)
            act.wait_ge(constants_in, 64)
            steps_of(act, run)

        @block.vector
        def _(dve):
            def rests(q, m, buf):
                dve.wait_ge(h_head, m * QUARTERS + q + 1)
                cut = slice(q * QB * D, (q + 1) * QB * D)
                for side in range(2):
                    here, there = slice(side * REST, side * REST + F), slice((1 - side) * REST, (1 - side) * REST + F)
                    src = misc[q % 2][here, 0:QB * 3 * D].rearrange("h (b l e) -> h b l e", b=QB, l=3)
                    head = hsplit[here, buf, side, :, cut].bitcast(F32).rearrange("h l (b e) -> h b l e", b=QB)
                    rest = hsplit[there, buf, side, :, cut].rearrange("h l (b e) -> h b l e", b=QB)
                    last = nc.vector.tensor_tensor(out=rest, in0=src[:, :, 0:2, :], in1=head, op=ALU.subtract)
                last.then_inc(h_rest, 1)

            def multiply(step, t):
                layer, j, u, us = step.unit(t)
                if layer == 1 and j == 0:
                    m = step.static
                    dve.wait_ge(x0rep_in[m % BUFS], (step.trip + m // BUFS + 1) * (16 * I1 * U1))
                if layer == 2 and j == 0:
                    dve.wait_ge(x1_copied, step.n * SPREADS)
                wait(dve, contracted, u - BUFS + 1)
                for side in range(2):
                    dve.wait_ge(spread, 2 * u + side + 1)
                    if layer == 1:
                        k, tiles = K1, I1
                        x = x0rep[:, step.static % BUFS, :, side * N:(side + 1) * N]
                    else:
                        k, tiles = K2, I2 - side * POOL_TILES
                        x = x1rep[:, side, 0:tiles, :]
                        if side == 1:
                            dve.wait_ge(hpool_copied, (step.n - 1) * J2 + j + 1)
                    h = rep_bank(us, side)[0:k, :].unsqueeze(1).to_broadcast([k, tiles, N])
                    nc.vector.tensor_tensor(out=prod[0:k, us % BUFS, side, 0:tiles, :], in0=h, in1=x, op=ALU.mult).then_inc(multiplied, 1)

            def by_row(ap):
                return ap.rearrange("p (b e) -> p b e", e=D)

            def take_x1(step):
                n = step.n
                dve.wait_ge(x1_head, n + 1)
                nc.vector.tensor_reduce(x1sum[:, bass.ds(n * SIDE_B, SIDE_B)], by_row(acc1), AX_X, ALU.add)
                for side in range(2):
                    here, there = slice(side * O, (side + 1) * O), slice((1 - side) * O, (2 - side) * O)
                    last = nc.vector.scalar_tensor_tensor(out=x1split[there, side, :], in0=acc1[here, :], scalar=cb1[here, :],
                                                          in1=x1split[here, side, :].bitcast(F32), op0=ALU.add, op1=ALU.subtract)
                last.then_inc(x1_rest, 1)

            def take_x2(m, end_of_units):
                dve.wait_ge(contracted, end_of_units)
                dve.wait_ge(g_copied, m + 1)
                nc.vector.scalar_tensor_tensor(out=x2g[:, :], in0=acc2[:, :], scalar=cb2, in1=g_sb[:, :],
                                               op0=ALU.add, op1=ALU.mult).then_inc(x2_taken, 1)
                dve.wait_ge(x2_taken, m + 1)
                nc.vector.tensor_reduce(ysum[:, bass.ds(m * SIDE_B, SIDE_B)], by_row(x2g[:, :]), AX_X, ALU.add).then_inc(prep, 1)

            def run(step, following):
                for t in range(UNITS):
                    if t in step.slots:
                        multiply(step, t)
                    if step.static == 0 and t == T_W3:
                        dve.wait_ge(w3_mult, 1)
                        for side in range(2):
                            rows_ = slice(side * REST, side * REST + F)
                            last = nc.vector.tensor_reduce(w3[rows_, side * O:(side + 1) * O], w3_stage()[rows_], AX_X, ALU.add)
                        last.then_inc(w3_done, 1)
                    if t == T_X2 and step.static >= 2:
                        take_x2(step.n - 2, step.before)
                    if T_H < t <= T_H + QUARTERS and step.has_h:
                        rests(t - 1 - T_H, step.n + 1, (step.static + 1) % BUFS)
                    if t == T_X1 and step.has1:
                        take_x1(step)

            nc.vector.memset(x0t_sb[D:D + 1, :, :].rearrange("p k n -> p (k n)"), 1.0).then_inc(zeros_done, 1)
            nc.vector.memset(hsplit[:, :, :, :, :].rearrange("p k s l n -> p (k s l n)").bitcast(F32), 0.0).then_inc(zeros_done, 1)
            nc.vector.memset(h3[:, :, :].rearrange("p k n -> p (k n)"), 0.0).then_inc(zeros_done, 1)
            nc.vector.memset(w3[:, :], 0.0).then_inc(zeros_done, 1)
            dve.wait_ge(weights_in, 32)
            nc.vector.tensor_copy(sel[:, :], sel_raw[:, :]).then_inc(sel_done, 1)
            dve.wait_ge(zeros_done, 4)
            for q in range(QUARTERS):
                rests(q, 0, 0)
            dve.wait_ge(constants_in, 64)
            nc.vector.tensor_tensor(out=const_row[:, :], in0=rows_sb[:, 0:O], in1=rows_sb[:, O:2 * O], op=ALU.mult).then_inc(sel_done, 1)
            dve.wait_ge(sel_done, 2)
            nc.vector.tensor_reduce(const_y[:, 0:1], const_row[:, :], AX_X, ALU.add).then_inc(sel_done, 1)
            dve.wait_ge(sel_done, 3)
            nc.vector.tensor_scalar(const_y[:, 1:2], const_y[:, 0:1], float(D), rows_sb[:, 2 * O:2 * O + 1], ALU.mult, ALU.add).then_inc(sel_done, 1)
            nc.vector.tensor_scalar(cb1d[:, :], cb1, float(D), None, ALU.mult).then_inc(sel_done, 1)
            steps_of(dve, run)
            last_step = Step(PAIRS, PAIRS)
            take_x2(PAIRS - 1, last_step.before + J2)
            dve.wait_ge(sel_done, 5)
            dve.wait_ge(x1_rest, PAIRS)
            nc.vector.tensor_scalar(x1tot[:, :], x1sum[:, :], cb1d[:, :], None, ALU.add).then_inc(prep, 1)
            dve.wait_ge(prep, PAIRS + 1)
            nc.vector.tensor_copy(const_row[:, 0:1], const_y[:, 1:2]).then_inc(sums_done, 1)
            dve.wait_ge(y_made, 1)
            dve.wait_ge(sums_done, 1)
            nc.vector.tensor_scalar(y_sb[:, :], misc[1][0:2, 0:PAIRS * SIDE_B], const_row[:, 0:1], None, ALU.add).then_inc(y_done, 1)

        @block.gpsimd
        def _(pool):
            stage = w3_stage()
            pool.wait_ge(w3_in, 64)
            nc.gpsimd.tensor_tensor(out=stage, in0=stage, in1=fc3_sb[:, :].unsqueeze(1).to_broadcast([KH, O, O]),
                                    op=ALU.mult).then_inc(w3_mult, 1)

            def run(step, following):
                if not step.has2:
                    return
                for t in step.slots:
                    layer, j, u, us = step.unit(t)
                    if layer == 1:
                        continue
                    if j == 0:
                        pool.wait_ge(x1_copied, step.n * SPREADS)
                    pool.wait_ge(contracted, u - BUFS + 1)
                    pool.wait_ge(hpool_copied, (step.n - 1) * J2 + j + 1)
                    h = hpool[:, j % 2, :].unsqueeze(1).to_broadcast([K2, POOL_TILES, N])
                    nc.gpsimd.tensor_tensor(out=prod[:, us % BUFS, 1, I2 - POOL_TILES:I2, :], in0=h,
                                            in1=x1rep[:, 1, I2 - POOL_TILES:I2, :], op=ALU.mult).then_inc(pool_multiplied, 1)

            steps_of(pool, run)


def kernel(**inputs):
    import concourse.bacc as bacc
    from concourse.bass_utils import run_bass_kernel_spmd

    p = {k: np.asarray(v) for k, v in inputs.items()}
    x0, fc = p["r_feature_emb"], p["L0_rec_fcW"]
    gw = np.concatenate([np.concatenate([p[f"L0_rec_gw{l}"], p[f"L0_rec_gb{l}"][None]], 0) for l in (1, 2, 3)], 1)
    w = p["L0_rec_cw1"].transpose(1, 2, 0)
    c1 = np.zeros((J1 * U1, I1, V1, O), np.float32)
    c1[:F, 0] = w[:, :V1]
    c1[:F, 1, 2 * V1 - F:] = w[:, V1:]
    c1 = c1.reshape(J1, U1, I1, V1, O).transpose(1, 3, 0, 2, 4).reshape(K1, -1)
    c2 = np.zeros((J2 * U2, I2, V2, O), np.float32)
    c2[:F] = p["L0_rec_cw2"].transpose(1, 2, 0).reshape(F, I2, V2, O)
    c2 = c2.reshape(J2, U2, I2, V2, O).transpose(1, 3, 0, 2, 4).reshape(K2, -1)
    cw3 = p["L0_rec_cw3"].transpose(1, 2, 0).reshape(F, -1)
    cols = np.zeros((128, 7), np.float32)
    for side in range(2):
        half = slice(side * O, (side + 1) * O)
        cols[half, 0], cols[half, 1], cols[half, 2] = p["L0_rec_cb1"], p["L0_rec_cb2"], fc[0, O:2 * O]
        cols[half, 3 + side], cols[half, 5 + side] = fc[0, :O], 1.0
    rows = np.stack([np.concatenate([fc[0, 2 * O:], p["L0_rec_cb3"], p["L0_rec_fcb"]])] * 2)
    sel1, sel2, sel_x = (np.zeros((128, n, k), np.float32) for n, k in ((J1, K1), (J2, K2), (I2, K2)))
    for h in range(F):
        for row in (h, REST + h):
            sel1[row, h // U1, (h % U1) * V1:(h % U1 + 1) * V1] = 1.0
            sel2[row, h // U2, (h % U2) * V2:(h % U2 + 1) * V2] = 1.0
    for m in range(O):
        for row in (m, REST + m):
            sel_x[row, m // V2, m % V2::V2] = 1.0
    sel = np.concatenate([a.reshape(128, -1) for a in (sel1, sel2, sel_x)], 1)
    arrays = {
        "x0t": x0.transpose(2, 0, 1).reshape(D, -1), "x0h": x0.transpose(1, 0, 2).reshape(F, -1), "gw": gw, "c1": c1,
        "c2": c2, "cw3": cw3, "fc3": fc[:, 2 * O:], "cols": cols, "rows": rows, "sel": sel,
    }
    arrays = {k: np.ascontiguousarray(v) for k, v in arrays.items()}
    nc = bacc.Bacc("TRN2", target_bir_lowering=False, num_devices=1)
    args = [nc.dram_tensor(f"{k}_dram", a.shape, mybir.dt.from_np(a.dtype), kind="ExternalInput").ap() for k, a in arrays.items()]
    y = nc.dram_tensor("y_dram", (B, 1), F32, kind="ExternalOutput").ap()
    cin_kernel(nc, *args, y)
    result = run_bass_kernel_spmd(nc, [{f"{k}_dram": a for k, a in arrays.items()}], core_ids=[0])
    return result.results[0]["y_dram"]
```

```python
from contextlib import ExitStack

import numpy as np

import concourse.bass as bass
from concourse import mybir

F32 = mybir.dt.float32
F32R = mybir.dt.float32r
ALU = mybir.AluOpType
ACT = mybir.ActivationFunctionType
AX_X = mybir.AxisListType.X

B, F, D = 512, 39, 64
O = 64
SIDE_B = 8
N = SIDE_B * D
PAIRS = B // (2 * SIDE_B)

U1, V1 = 6, 20
J1, I1 = -(-F // V1), -(-F // U1)
GROUPS = ((0, 4), (4, 3))
GROUP = 4
U2, V2 = 8, 16
J2, I2 = -(-F // U2), O // V2
K1, K2 = U1 * V1, U2 * V2
REST = 64
KH = REST + F
POOL_TILES = 2

UNITS1, UNITS2 = len(GROUPS) * J1, J2
ORDER = [(1, k) for k in range(UNITS1)] + [(2, k) for k in range(UNITS2)]
UNITS = len(ORDER)
SPREAD_SLOTS = [(j * len(GROUPS), (j + 1) * len(GROUPS) - 1) for j in range(J1)] + [(t, t) for t in range(UNITS1, UNITS)]
RING = 5
AHEAD = 2
T_X2 = 1
T_X1SUM = 2
T_H = (0, 2, 4, 5)
T_G = 7
T_X0 = 3
T_W3 = (1, 3)
T_LAST1 = UNITS1 - 1
SEL = J1 * K1 + J2 * K2
QUARTERS = 4
QB = SIDE_B // QUARTERS
X1_READS = U2
BUFS = 3
assert UNITS % BUFS == 0 and UNITS1 + UNITS2 == UNITS


def tiles_of(layer, number):
    if layer == 2:
        return number, 0, I2
    j, group = divmod(number, len(GROUPS))
    return j, *GROUPS[group]


class Step:

    def __init__(self, n, static, trip=0):
        self.n, self.static, self.trip = n, static, trip
        self.has1 = static < PAIRS
        self.has2 = static >= 1
        self.has_h = 1 <= static < PAIRS - 1
        self.slots = [t for t, (layer, _) in enumerate(ORDER) if (layer == 1 and self.has1) or (layer == 2 and self.has2)]
        self.spreads = [w for w, (first, _) in enumerate(SPREAD_SLOTS) if first in self.slots]
        self.before = 0 if static == 0 else (n - 1) * UNITS + UNITS1
        self.spreads_before = 0 if static == 0 else (n - 1) * len(SPREAD_SLOTS) + J1

    def back(self):
        return Step(self.n - 1, self.static - 1, self.trip)

    def number(self, t):
        return self.before + self.slots.index(t)

    def product_buffer(self, t):
        return Step(self.static, self.static).number(t) % BUFS

    def spread_number(self, w):
        return self.spreads_before + self.spreads.index(w)

    def hpool_buffer(self, w):
        return Step(self.static, self.static).spread_number(w) % BUFS


def spread_of(t):
    return next(w for w, (first, last) in enumerate(SPREAD_SLOTS) if first <= t <= last)


def spread_ahead(step, following, t):
    k = step.slots.index(t) + AHEAD
    if k >= len(step.slots):
        if following is None:
            return None
        k, step = k - len(step.slots), following
    first = step.slots[k]
    w = spread_of(first)
    return (step, w) if SPREAD_SLOTS[w][0] == first else None


def last_user(step, w, side):
    wanted = (2 * w + side) % RING
    sides = [(step, v, s) for v in step.spreads for s in range(2) if (v, s) < (w, side)]
    if step.static:
        back = step.back()
        sides = [(back, v, s) for v in back.spreads for s in range(2)] + sides
    same = [(st, SPREAD_SLOTS[v][1], s) for st, v, s in sides if (2 * v + s) % RING == wanted]
    return same[-1] if same else None


def last_hpool_user(step, w):
    spreads = [(step, v) for v in step.spreads if v < w]
    if step.static:
        back = step.back()
        spreads = [(back, v) for v in back.spreads] + spreads
    return (spreads[-BUFS][0], SPREAD_SLOTS[spreads[-BUFS][1]][1]) if len(spreads) >= BUFS else None


def steps_of(eng, run, last=PAIRS):
    first = 2
    for n in range(first):
        run(Step(n, n), Step(n + 1, n + 1))
    trips = (PAIRS - 1 - first) // BUFS
    with eng.Fori(0, trips) as trip:
        for k in range(BUFS):
            n = first + k
            run(Step(trip * BUFS + n, n, trip), Step(trip * BUFS + n + 1, n + 1, trip))
    for n in range(first + trips * BUFS, last + 1):
        run(Step(n, n), Step(n + 1, n + 1) if n < PAIRS else None)


def wait(eng, sem, value):
    if not isinstance(value, int) or value > 0:
        eng.wait_ge(sem, value)


def cin_kernel(nc, x0t, x0h, gw, c1_in, c2_in, cw3, cols, rows, sel_in, x1_dram, out):
    with ExitStack() as ctx:
        def sb(name, shape, dt=F32):
            return ctx.enter_context(nc.sbuf_tensor(name, shape, dt))

        def sem(name):
            return ctx.enter_context(nc.semaphore(name))

        x0t_sb = sb("x0t_sb", [D, BUFS, 2 * SIDE_B * F])
        x0split = sb("x0split", [2 * D, BUFS, SIDE_B, 2 * REST], F32R)
        x0rep = sb("x0rep", [128, BUFS, GROUP, 2 * N])
        gw_sb = sb("gw_sb", [2 * D, 3 * D])
        gwsplit = sb("gwsplit", [2 * D, 2, 3 * D], F32R)
        gb_sb = sb("gb_sb", [1, 3 * D])
        gbsplit = sb("gbsplit", [REST + 1, 3 * D], F32R)
        ones = sb("ones", [REST + 1, KH], F32R)
        c1 = sb("c1", [K1, J1, I1, O])
        c2 = sb("c2", [K2, J2, I2, O])
        w3 = sb("w3", [KH, 2 * O])
        w3t = sb("w3t", [O, F])
        cols_sb = sb("cols_sb", [128, 8])
        rows_sb = sb("rows_sb", [2, 2 * O + 1])
        sel_raw = sb("sel_raw", [128, SEL + O])
        sel = sb("sel", [128, SEL], F32R)
        hsplit = sb("hsplit", [128, BUFS, 2, 2, N], F32R)
        h3 = sb("h3", [KH, BUFS, N])
        x1_sb = sb("x1_sb", [128, N])
        x1rep = sb("x1rep", [K2, I2, 2 * N])
        hpool = sb("hpool", [K2, BUFS, N])
        prod = sb("prod", [128, BUFS, 2, I2, N])
        g_sb = sb("g_sb", [128, N])
        x2g = sb("x2g", [128, N])
        x1sum = sb("x1sum", [128, PAIRS * SIDE_B])
        ysum = sb("ysum", [128, PAIRS * SIDE_B])
        const_row = sb("const_row", [2, O])
        const_y = sb("const_y", [2, 2])
        y_sb = sb("y_sb", [2, PAIRS * SIDE_B])

        ps = ctx.enter_context(nc.psum_tensor("ps", [128, 8, N], F32))
        ring, misc, acc1, acc2 = [ps[:, k, :] for k in range(RING)], ps[:, 5, :], ps[:, 6, :], ps[:, 7, :]

        cb1, cb2, fc2 = cols_sb[:, 0:1], cols_sb[:, 1:2], cols_sb[:, 2:3]
        fc1_sides, one_sides = cols_sb[:, 3:5], cols_sb[:, 5:7]
        sel1 = sel[:, 0:J1 * K1].rearrange("k (j p) -> k j p", j=J1)
        sel2 = sel[:, J1 * K1:J1 * K1 + J2 * K2].rearrange("k (j p) -> k j p", j=J2)
        fc3, ident = cols_sb[0:O, 7:8], sel_raw[0:O, SEL:SEL + O]

        gw_in = sem("gw_in")
        gw_head = sem("gw_head")
        gw_rest = sem("gw_rest")
        x0_head = sem("x0_head")
        x0_rest = sem("x0_rest")
        sel_in_1 = sem("sel_in_1")
        sel_in_2 = sem("sel_in_2")
        c1_loaded = sem("c1_loaded")
        cols_in = sem("cols_in")
        c2_rows_in = sem("c2_rows_in")
        w3_in = sem("w3_in")
        x0t_in = [sem(f"x0t_in{k}") for k in range(BUFS)]
        x0rep_in = [sem(f"x0rep_in{k}") for k in range(BUFS)]
        zeros_first = sem("zeros_first")
        zeros_rest = sem("zeros_rest")
        sel_done = sem("sel_done")
        w3_flat = sem("w3_flat")
        w3_flat_copied = sem("w3_flat_copied")
        w3_turned = sem("w3_turned")
        w3_done = sem("w3_done")
        h_made = sem("h_made")
        h_head = sem("h_head")
        h_rest = sem("h_rest")
        spread = sem("spread")
        hpool_copied = sem("hpool_copied")
        multiplied = sem("multiplied")
        pool_multiplied = sem("pool_multiplied")
        contracted = sem("contracted")
        x1_taken = sem("x1_taken")
        x1_stored = sem("x1_stored")
        x1_spread = sem("x1_spread")
        x1_summed = sem("x1_summed")
        g_made = sem("g_made")
        g_copied = sem("g_copied")
        x2_taken = sem("x2_taken")
        tables_loaded = sem("tables_loaded")
        const_steps = sem("const_steps")
        ysum_done = sem("ysum_done")
        y_made = sem("y_made")
        y_done = sem("y_done")
        y_out = sem("y_out")

        first_banks = (ring[0:4], (misc, acc1, ring[4], misc))
        w3_bank = ring[4]

        def acc1_of(step):
            return acc1 if step.static else acc2

        def acc2_of(step):
            return acc2 if step.static < PAIRS else acc1

        def x0_by_row(ap):
            return ap.rearrange("e b (s f) -> e s b f", s=2)[:, :, :, 0:F]

        def group_buffer(static, group):
            return (len(GROUPS) * static + group) % BUFS

        def x0_tiles(eng, step, number):
            j, group = divmod(number, len(GROUPS))
            if j == 0:
                loads = step.trip * len(GROUPS) + (len(GROUPS) * step.static + group) // BUFS + 1
                eng.wait_ge(x0rep_in[group_buffer(step.static, group)], loads * (16 * U1))
            return x0rep[0:K1, group_buffer(step.static, group), 0:GROUPS[group][1], :]

        def x1_buffer(step):
            return x1rep[:, :, :] if step.static < PAIRS else x0rep[:, group_buffer(PAIRS, 0), :, :]

        def x1_tiles(eng, step, number):
            if number == 0:
                eng.wait_ge(x1_spread, step.n * (16 * X1_READS))
            return x1_buffer(step)

        block = ctx.enter_context(nc.Block())

        @block.sync
        def _(sp):
            def load_x0t(m, buf):
                sp.dma_start(x0t_sb[:, buf, :], x0t[:, bass.ds(m * (2 * SIDE_B * F), 2 * SIDE_B * F)]).then_inc(x0t_in[buf], 16)

            def load_group(m, static, group):
                i0, tiles = GROUPS[group]
                buf = group_buffer(static, group)
                for u in range(U1):
                    row = x0h[u:u + 1, bass.ds(m * (I1 * 2 * N) + i0 * (2 * N), tiles * (2 * N))]
                    sp.dma_start(x0rep[u * V1:(u + 1) * V1, buf, 0:tiles, :].rearrange("p i n -> p (i n)"),
                                 row.to_broadcast([V1, tiles * 2 * N])).then_inc(x0rep_in[buf], 16)

            def after_unit(step, t):
                sp.wait_ge(multiplied, 2 * (step.number(t) + 1))
                sp.wait_ge(pool_multiplied, step.number(t) + 1)

            def run(step, following):
                n, static = step.n, step.static
                reads_before, stores = n * (16 * X1_READS), (n + 1) * 32
                if not isinstance(n, int):
                    sp.compute_val(reads_before)
                    sp.compute_val(stores)
                if static + 2 < PAIRS:
                    wait(sp, x0_rest, n)
                    load_x0t(n + 2, (static + 2) % BUFS)
                if static + 1 < PAIRS:
                    after_unit(step, T_LAST1 - 1)
                    load_group(n + 1, static + 1, 1)
                if static + 2 < PAIRS:
                    after_unit(step, T_LAST1)
                    load_group(n + 2, static + 2, 0)
                sp.wait_ge(x1_taken, n + 1)
                wait(sp, x1_spread, reads_before)
                for side in range(2):
                    sp.dma_start(x1_dram[:, side * N:(side + 1) * N], x1_sb[side * O:(side + 1) * O, :]).then_inc(x1_stored, 16)
                if static == 0:
                    sp.wait_ge(w3_flat, 1)
                elif static < PAIRS - 1:
                    after_unit(step, UNITS - 1)
                else:
                    after_unit(step.back(), T_LAST1)
                sp.wait_ge(x1_stored, stores)
                by_m = x1_dram.rearrange("(i v) n -> v i n", v=V2)
                for u in range(X1_READS):
                    sp.dma_start(x1_buffer(following)[u * V2:(u + 1) * V2, :, :], by_m).then_inc(x1_spread, 16)

            for half in range(2):
                sp.dma_start(gw_sb[half * D:(half + 1) * D, :], gw[0:D, :]).then_inc(gw_in, 16)
            load_x0t(0, 0)
            sp.dma_start(gb_sb[:, :], gw[D:D + 1, :]).then_inc(gw_in, 16)
            load_x0t(1, 1)
            first = J1 * K1
            sp.dma_start(sel_raw[:, 0:first], sel_in[:, 0:first]).then_inc(sel_in_1, 16)
            load_group(0, 0, 0)
            sp.dma_start(c1[:, :, :, :].rearrange("p j i o -> p (j i o)"), c1_in[:, :]).then_inc(c1_loaded, 16)
            sp.dma_start(cols_sb[:, :], cols[:, :]).then_inc(cols_in, 16)
            load_group(0, 0, 1)
            sp.dma_start(x1rep[0:O, :, :].rearrange("p i n -> p (i n)")[:, 0:F * O], cw3[:, :]).then_inc(w3_in, 16)
            sp.dma_start(sel_raw[:, first:], sel_in[:, first:]).then_inc(sel_in_2, 16)
            load_group(1, 1, 0)
            sp.dma_start(c2[:, :, :, :].rearrange("p j i o -> p (j i o)"), c2_in[:, :]).then_inc(c2_rows_in, 16)
            sp.dma_start(rows_sb[:, :], rows[:, :]).then_inc(c2_rows_in, 16)
            steps_of(sp, run, PAIRS - 1)
            sp.wait_ge(y_done, 1)
            sp.dma_start(out.rearrange("(n s b) o -> s n (b o)", s=2, b=SIDE_B),
                         y_sb[:, :].rearrange("s (n b) -> s n b", b=SIDE_B)).then_inc(y_out, 16)
            sp.wait_ge(y_out, 16)

        @block.tensor
        def _(pe):
            def make_h(q, bank, m, buf):
                if q == 0:
                    pe.wait_ge(x0_rest, m + 1)
                for b in range(QB):
                    nc.tensor.matmul(bank[0:KH, b * 3 * D:(b + 1) * 3 * D], ones[:, :], gbsplit[:, :], start=True, stop=False)
                    for part in range(2):
                        last = nc.tensor.matmul(bank[0:KH, b * 3 * D:(b + 1) * 3 * D], x0split[:, buf, q * QB + b, 0:KH],
                                                gwsplit[:, part, :], start=False, stop=(part == 1))
                last.then_inc(h_made, 1)

            def spread_h(step, w):
                first, _ = SPREAD_SLOTS[w]
                layer, number = ORDER[first]
                pair_static = step.static if layer == 1 else step.static - 1
                if first == 0:
                    pe.wait_ge(h_rest, (step.n + 1) * QUARTERS)
                if step.static == 1 and layer == 2 and number == 0:
                    pe.wait_ge(w3_done, 1)
                j, k = tiles_of(layer, number)[0], (K1, K2)[layer - 1]
                lhs = (sel1, sel2)[layer - 1][0:KH, j, :]
                for side in range(2):
                    user = last_user(step, w, side)
                    if user:
                        user_step, user_slot, user_side = user
                        pe.wait_ge(multiplied, 2 * user_step.number(user_slot) + user_side + 1)
                    nc.tensor.matmul(ring[(2 * w + side) % RING][0:k, :], lhs, hsplit[0:KH, pair_static % BUFS, side, layer - 1, :],
                                     start=True, stop=True).then_inc(spread, 1)

            def contract(step, t):
                layer, number = ORDER[t]
                j, i0, tiles = tiles_of(layer, number)
                acc, c, k, units = (acc1_of(step), c1, K1, UNITS1) if layer == 1 else (acc2_of(step), c2, K2, UNITS2)
                if number == 0:
                    if layer == 1:
                        wait(pe, x1_taken, step.n if step.static >= 2 else 0)
                    elif step.static == 1:
                        pe.wait_ge(x1_taken, 1)
                    elif step.static < PAIRS:
                        pe.wait_ge(x2_taken, step.n - 1)
                    else:
                        pe.wait_ge(x1_taken, PAIRS)
                pe.wait_ge(multiplied, 2 * (step.number(t) + 1))
                for i in range(tiles):
                    if i == tiles - POOL_TILES:
                        pe.wait_ge(pool_multiplied, step.number(t) + 1)
                    for side in range(2):
                        last = nc.tensor.matmul(acc[side * O:(side + 1) * O, :], c[:, j, i0 + i, :],
                                                prod[0:k, step.product_buffer(t), side, i, :],
                                                start=(number == 0 and i == 0), stop=(number == units - 1 and i == tiles - 1))
                last.then_inc(contracted, 1)

            def make_w3(t):
                if t == T_W3[0]:
                    pe.wait_ge(w3_in, 16)
                    pe.wait_ge(cols_in, 16)
                    cw3_rows = x1rep[0:O, :, :].rearrange("p i n -> p (i n)")
                    pe.wait_ge(h_rest, QUARTERS + 3)
                    for h in range(F):
                        last = nc.tensor.matmul(w3_bank[0:O, h:h + 1], cw3_rows[:, h * O:(h + 1) * O], fc3, start=True, stop=True)
                    last.then_inc(w3_flat, 1)
                elif t == T_W3[1]:
                    pe.wait_ge(w3_flat_copied, 1)
                    pe.wait_ge(sel_in_2, 16)
                    pe.wait_ge(sel_done, 2)
                    pe.wait_ge(c2_rows_in, 32)
                    for side in range(2):
                        last = nc.tensor.matmul(w3_bank[side * REST:side * REST + F, O:2 * O], w3t[:, :], ident, start=True, stop=True)
                    last.then_inc(w3_turned, 1)

            def run(step, following):
                n = step.n
                for t in step.slots:
                    found = spread_ahead(step, following, t)
                    if found:
                        spread_h(*found)
                    if t == T_G and step.has2:
                        if step.has_h:
                            pe.wait_ge(h_rest, (n + 2) * QUARTERS)
                        else:
                            pe.wait_ge(g_copied, n - 1)
                        nc.tensor.matmul(misc, w3[:, :], h3[0:KH, (step.static - 1) % BUFS, :],
                                         start=True, stop=True).then_inc(g_made, 1)
                    if t in T_H and step.has_h:
                        q = T_H.index(t)
                        if q == 0:
                            wait(pe, g_copied, n - 1)
                        else:
                            pe.wait_ge(h_rest, (n + 1) * QUARTERS + q)
                        make_h(q, misc, n + 1, (step.static + 1) % BUFS)
                    contract(step, t)
                    if step.static == 0:
                        if t == 0:
                            pe.wait_ge(h_rest, QUARTERS + 1)
                            make_h(QUARTERS - 1, first_banks[1][-1], 1, 1)
                        make_w3(t)

            pe.wait_ge(gw_rest, 2)
            for q in range(QUARTERS):
                make_h(q, first_banks[0][q], 0, 0)

            make_h(0, first_banks[1][0], 1, 1)
            pe.wait_ge(sel_done, 1)
            spread_h(Step(0, 0), 0)
            for q in range(1, QUARTERS - 1):
                make_h(q, first_banks[1][q], 1, 1)
            pe.wait_ge(c1_loaded, 16)
            steps_of(pe, run)
            pe.wait_ge(g_copied, PAIRS)
            pe.wait_ge(x1_summed, PAIRS)
            nc.tensor.matmul(misc[0:2, 0:PAIRS * SIDE_B], fc1_sides, x1sum[:, :], start=True, stop=False)
            pe.wait_ge(ysum_done, PAIRS)
            nc.tensor.matmul(misc[0:2, 0:PAIRS * SIDE_B], one_sides, ysum[:, :], start=False, stop=True).then_inc(y_made, 1)

        @block.scalar
        def _(act):
            def heads(q, bank, m, buf):
                act.wait_ge(h_made, m * QUARTERS + q + 1)
                cut = slice(q * QB * D, (q + 1) * QB * D)
                for side in range(2):
                    rows_ = slice(side * REST, side * REST + F)
                    src = bank[rows_, 0:QB * 3 * D].rearrange("h (b l e) -> h b l e", b=QB, l=3)
                    dst = hsplit[rows_, buf, side, :, cut].rearrange("h l (b e) -> h b l e", b=QB)
                    nc.scalar.copy(dst, src[:, :, 0:2, :])
                    last = nc.scalar.copy(h3[rows_, buf, cut].rearrange("h (b e) -> h b e", b=QB), src[:, :, 2, :])
                last.then_inc(h_head, 1)

            def head_x0(m, static, trip):
                buf = static % BUFS
                act.wait_ge(x0t_in[buf], (trip + static // BUFS + 1) * 16)
                wait(act, h_made, (m - BUFS + 1) * QUARTERS if static >= BUFS else 0)
                nc.scalar.copy(x0_by_row(x0split[0:D, buf, :, :]), x0t_sb[:, buf, :].rearrange("e (s b f) -> e s b f", s=2, f=F)).then_inc(x0_head, 1)

            def copy_for_pool(step, w):
                k = (K1, K2)[ORDER[SPREAD_SLOTS[w][0]][0] - 1]
                act.wait_ge(spread, 2 * (step.spread_number(w) + 1))
                user = last_hpool_user(step, w)
                if user:
                    user_step, user_slot = user
                    act.wait_ge(pool_multiplied, user_step.number(user_slot) + 1)
                nc.scalar.copy(hpool[0:k, step.hpool_buffer(w), :], ring[(2 * w + 1) % RING][0:k, :]).then_inc(hpool_copied, 1)

            def run(step, following):
                n = step.n
                for t in step.slots:
                    found = spread_ahead(step, following, t)
                    if found:
                        copy_for_pool(*found)
                    if t == T_G and step.has2:
                        act.wait_ge(g_made, n)
                        wait(act, x2_taken, n - 1)
                        nc.scalar.activation(g_sb[:, :], misc, ACT.Identity, bias=fc2).then_inc(g_copied, 1)
                    if t == T_X0 and step.static + 2 < PAIRS:
                        head_x0(n + 2, step.static + 2, step.trip)
                    if t in T_H and step.has_h:
                        heads(T_H.index(t), misc, n + 1, (step.static + 1) % BUFS)
                    if t == 0 and step.static == 0:
                        heads(QUARTERS - 1, first_banks[1][-1], 1, 1)
                    if t == T_LAST1:
                        act.wait_ge(contracted, step.number(T_LAST1) + 1)
                        wait(act, x1_stored, n * 32)
                        wait(act, x1_summed, n)
                        nc.scalar.activation(x1_sb[:, :], acc1_of(step), ACT.Identity, bias=cb1).then_inc(x1_taken, 1)

            act.wait_ge(zeros_first, 2)
            nc.scalar.copy(x2g[0:1, 0:1], ones[0:1, 0:1].bitcast(F32)).then_inc(tables_loaded, 1)
            act.wait_ge(gw_in, 48)
            act.wait_ge(zeros_first, 3)
            nc.scalar.copy(gwsplit[:, 0, :], gw_sb[:, :]).then_inc(gw_head, 1)
            nc.scalar.copy(gbsplit[0:1, :], gb_sb[:, :]).then_inc(gw_head, 1)
            head_x0(0, 0, 0)
            head_x0(1, 1, 0)
            act.wait_ge(zeros_first, 6)
            for q in range(QUARTERS):
                heads(q, first_banks[0][q], 0, 0)
            act.wait_ge(zeros_rest, 2)
            heads(0, first_banks[1][0], 1, 1)
            copy_for_pool(Step(0, 0), 0)
            for q in range(1, QUARTERS - 1):
                heads(q, first_banks[1][q], 1, 1)
            act.wait_ge(cols_in, 16)
            steps_of(act, run)

        @block.vector
        def _(dve):
            def rests(q, bank, m, buf):
                dve.wait_ge(h_head, m * QUARTERS + q + 1)
                cut = slice(q * QB * D, (q + 1) * QB * D)
                for side in range(2):
                    here, there = slice(side * REST, side * REST + F), slice((1 - side) * REST, (1 - side) * REST + F)
                    src = bank[here, 0:QB * 3 * D].rearrange("h (b l e) -> h b l e", b=QB, l=3)
                    head = hsplit[here, buf, side, :, cut].bitcast(F32).rearrange("h l (b e) -> h b l e", b=QB)
                    rest = hsplit[there, buf, side, :, cut].rearrange("h l (b e) -> h b l e", b=QB)
                    last = nc.vector.tensor_tensor(out=rest, in0=src[:, :, 0:2, :], in1=head, op=ALU.subtract)
                last.then_inc(h_rest, 1)

            def rest_x0(m, buf):
                dve.wait_ge(x0_head, m + 1)
                nc.vector.tensor_tensor(out=x0_by_row(x0split[D:2 * D, buf, :, :]),
                                        in0=x0t_sb[:, buf, :].rearrange("e (s b f) -> e s b f", s=2, f=F),
                                        in1=x0_by_row(x0split[0:D, buf, :, :].bitcast(F32)), op=ALU.subtract).then_inc(x0_rest, 1)

            def multiply(step, t):
                layer, number = ORDER[t]
                j, i0, tiles = tiles_of(layer, number)
                k, w = (K1, K2)[layer - 1], spread_of(t)
                if layer == 1:
                    x = x0_tiles(dve, step, number)
                else:
                    x = x1_tiles(dve, step, number)
                wait(dve, contracted, step.number(t) - BUFS + 1)
                for side in range(2):
                    own = tiles - side * POOL_TILES
                    if t == SPREAD_SLOTS[w][0]:
                        dve.wait_ge(spread, 2 * step.spread_number(w) + side + 1)
                        if side == 1:
                            dve.wait_ge(hpool_copied, step.spread_number(w) + 1)
                    h = ring[(2 * w + side) % RING][0:k, :].unsqueeze(1).to_broadcast([k, own, N])
                    nc.vector.tensor_tensor(out=prod[0:k, step.product_buffer(t), side, 0:own, :], in0=h,
                                            in1=x[:, 0:own, side * N:(side + 1) * N], op=ALU.mult).then_inc(multiplied, 1)

            def by_row(ap):
                return ap.rearrange("p (b e) -> p b e", e=D)

            def sum_x1(m):
                dve.wait_ge(x1_taken, m + 1)
                nc.vector.tensor_reduce(x1sum[:, bass.ds(m * SIDE_B, SIDE_B)], by_row(x1_sb[:, :]), AX_X, ALU.add).then_inc(x1_summed, 1)

            def take_x2(m, acc, end_of_units):
                dve.wait_ge(contracted, end_of_units)
                dve.wait_ge(g_copied, m + 1)
                nc.vector.scalar_tensor_tensor(out=x2g[:, :], in0=acc[:, :], scalar=cb2, in1=g_sb[:, :],
                                               op0=ALU.add, op1=ALU.mult).then_inc(x2_taken, 1)
                dve.wait_ge(x2_taken, m + 1)
                nc.vector.tensor_reduce(ysum[:, bass.ds(m * SIDE_B, SIDE_B)], by_row(x2g[:, :]), AX_X, ALU.add).then_inc(ysum_done, 1)

            def first_extras(t):
                if t == 0:
                    dve.wait_ge(zeros_rest, 2)
                    rests(0, first_banks[1][0], 1, 1)
                    rests(1, first_banks[1][1], 1, 1)
                if t == 1:
                    for q in range(2, QUARTERS):
                        rests(q, first_banks[1][q], 1, 1)
                    dve.wait_ge(sel_in_2, 16)
                    nc.vector.tensor_copy(sel[:, J1 * K1:], sel_raw[:, J1 * K1:SEL]).then_inc(sel_done, 1)
                if t == T_X0:
                    rest_x0(2, 2)
                if t == T_W3[1]:
                    dve.wait_ge(w3_flat, 1)
                    nc.vector.tensor_copy(w3t[:, :], w3_bank[0:O, 0:F]).then_inc(w3_flat_copied, 1)
                if t == T_LAST1:
                    dve.wait_ge(cols_in, 16)
                    dve.wait_ge(c2_rows_in, 32)
                    nc.vector.tensor_tensor(out=const_row[:, :], in0=rows_sb[:, 0:O], in1=rows_sb[:, O:2 * O], op=ALU.mult).then_inc(const_steps, 1)
                    dve.wait_ge(const_steps, 1)
                    nc.vector.tensor_reduce(const_y[:, 0:1], const_row[:, :], AX_X, ALU.add).then_inc(const_steps, 1)
                    dve.wait_ge(const_steps, 2)
                    nc.vector.tensor_scalar(const_y[:, 1:2], const_y[:, 0:1], float(D), rows_sb[:, 2 * O:2 * O + 1],
                                            ALU.mult, ALU.add).then_inc(const_steps, 1)

            def run(step, following):
                late = 0 if step.has1 else UNITS1
                for t in step.slots:
                    multiply(step, t)
                    if step.static == 0:
                        first_extras(t)
                    if step.static == 1 and t == 1:
                        dve.wait_ge(w3_turned, 1)
                        for side in range(2):
                            rows_ = slice(side * REST, side * REST + F)
                            last = nc.vector.tensor_copy(w3[rows_, side * O:(side + 1) * O], w3_bank[rows_, O:2 * O])
                        last.then_inc(w3_done, 1)
                    if t == T_X2 + late and step.static >= 2:
                        take_x2(step.n - 2, acc2, step.before)
                    if t == T_X1SUM + late and step.has2:
                        sum_x1(step.n - 1)
                    if t == T_X0 + 1 and step.static >= 1 and step.static + 2 < PAIRS:
                        rest_x0(step.n + 2, (step.static + 2) % BUFS)
                    if t - 1 in T_H and step.has_h:
                        rests(T_H.index(t - 1), misc, step.n + 1, (step.static + 1) % BUFS)

            nc.vector.memset(gbsplit[:, :].bitcast(F32), 0.0).then_inc(zeros_first, 1)
            nc.vector.memset(ones[:, :].bitcast(F32), 1.0).then_inc(zeros_first, 1)
            nc.vector.memset(x0split[:, :, :, F:REST].rearrange("p k b n -> p (k b) n").bitcast(F32), 0.0).then_inc(zeros_first, 1)
            nc.vector.memset(hsplit[:, 0, :, :, :].rearrange("p s l n -> p (s l n)").bitcast(F32), 0.0).then_inc(zeros_first, 1)
            nc.vector.memset(h3[:, 0, :], 0.0).then_inc(zeros_first, 1)
            nc.vector.memset(w3[:, :], 0.0).then_inc(zeros_first, 1)
            dve.wait_ge(gw_head, 2)
            nc.vector.tensor_tensor(out=gwsplit[:, 1, :], in0=gw_sb[:, :], in1=gwsplit[:, 0, :].bitcast(F32), op=ALU.subtract).then_inc(gw_rest, 1)
            nc.vector.tensor_tensor(out=gbsplit[REST:REST + 1, :], in0=gb_sb[:, :], in1=gbsplit[0:1, :].bitcast(F32),
                                    op=ALU.subtract).then_inc(gw_rest, 1)
            rest_x0(0, 0)
            rest_x0(1, 1)
            dve.wait_ge(sel_in_1, 16)
            nc.vector.tensor_copy(sel[:, 0:J1 * K1], sel_raw[:, 0:J1 * K1]).then_inc(sel_done, 1)
            dve.wait_ge(zeros_first, 6)
            for q in range(QUARTERS):
                rests(q, first_banks[0][q], 0, 0)
            steps_of(dve, run)
            last_step = Step(PAIRS, PAIRS)
            take_x2(PAIRS - 1, acc2_of(last_step), last_step.before + UNITS2)
            dve.wait_ge(const_steps, 3)
            dve.wait_ge(y_made, 1)
            nc.vector.tensor_scalar(y_sb[:, :], misc[0:2, 0:PAIRS * SIDE_B], const_y[:, 1:2], None, ALU.add).then_inc(y_done, 1)

        @block.gpsimd
        def _(pool):
            nc.gpsimd.memset(hsplit[:, 1:BUFS, :, :, :].rearrange("p k s l n -> p (k s l n)").bitcast(F32), 0.0).then_inc(zeros_rest, 1)
            nc.gpsimd.memset(h3[:, 1:BUFS, :].rearrange("p k n -> p (k n)"), 0.0).then_inc(zeros_rest, 1)

            def run(step, following):
                for t in step.slots:
                    layer, number = ORDER[t]
                    j, i0, tiles = tiles_of(layer, number)
                    k, w = (K1, K2)[layer - 1], spread_of(t)
                    if layer == 1:
                        x = x0_tiles(pool, step, number)
                    else:
                        x = x1_tiles(pool, step, number)
                    wait(pool, contracted, step.number(t) - BUFS + 1)
                    if t == SPREAD_SLOTS[w][0]:
                        pool.wait_ge(hpool_copied, step.spread_number(w) + 1)
                    h = hpool[0:k, step.hpool_buffer(w), :].unsqueeze(1).to_broadcast([k, POOL_TILES, N])
                    own = slice(tiles - POOL_TILES, tiles)
                    nc.gpsimd.tensor_tensor(out=prod[0:k, step.product_buffer(t), 1, own, :], in0=h,
                                            in1=x[:, own, N:2 * N], op=ALU.mult).then_inc(pool_multiplied, 1)

            steps_of(pool, run)


def kernel(**inputs):
    import concourse.bacc as bacc
    from concourse.bass_utils import run_bass_kernel_spmd

    p = {k: np.asarray(v) for k, v in inputs.items()}
    x0, fc = p["r_feature_emb"], p["L0_rec_fcW"]
    gw = np.concatenate([np.concatenate([p[f"L0_rec_gw{l}"], p[f"L0_rec_gb{l}"][None]], 0) for l in (1, 2, 3)], 1)
    w = p["L0_rec_cw1"].transpose(1, 2, 0)
    c1 = np.zeros((J1 * V1, I1 * U1, O), np.float32)
    c1[:F, :F] = w
    c1 = c1.reshape(J1, V1, I1, U1, O).transpose(3, 1, 0, 2, 4).reshape(K1, -1)
    x0h = np.zeros((I1 * U1, B * D), np.float32)
    x0h[:F] = x0.transpose(1, 0, 2).reshape(F, -1)
    x0h = x0h.reshape(I1, U1, PAIRS, 2 * N).transpose(1, 2, 0, 3).reshape(U1, -1)
    c2 = np.zeros((J2 * U2, I2, V2, O), np.float32)
    c2[:F] = p["L0_rec_cw2"].transpose(1, 2, 0).reshape(F, I2, V2, O)
    c2 = c2.reshape(J2, U2, I2, V2, O).transpose(1, 3, 0, 2, 4).reshape(K2, -1)
    cols = np.zeros((128, 8), np.float32)
    cols[:O, 7] = fc[0, 2 * O:]
    for side in range(2):
        half = slice(side * O, (side + 1) * O)
        cols[half, 0], cols[half, 1], cols[half, 2] = p["L0_rec_cb1"], p["L0_rec_cb2"], fc[0, O:2 * O]
        cols[half, 3 + side], cols[half, 5 + side] = fc[0, :O], 1.0
    rows = np.stack([np.concatenate([fc[0, 2 * O:], p["L0_rec_cb3"], p["L0_rec_fcb"]])] * 2)
    sel1, sel2 = (np.zeros((128, n, k), np.float32) for n, k in ((J1, K1), (J2, K2)))
    for h in range(F):
        for row in (h, REST + h):
            sel1[row, h // V1, h % V1::V1] = 1.0
            sel2[row, h // U2, (h % U2) * V2:(h % U2 + 1) * V2] = 1.0
    sel = np.concatenate([a.reshape(128, -1) for a in (sel1, sel2)] + [np.eye(128, O, dtype=np.float32)], 1)
    x0t = x0.transpose(2, 0, 1).reshape(D, -1)
    arrays = {
        "x0t": x0t, "x0h": x0h, "gw": gw, "c1": c1,
        "c2": c2, "cw3": p["L0_rec_cw3"].reshape(O, -1), "cols": cols, "rows": rows, "sel": sel,
    }
    arrays = {k: np.ascontiguousarray(v) for k, v in arrays.items()}
    nc = bacc.Bacc("TRN2", target_bir_lowering=False, num_devices=1)
    args = [nc.dram_tensor(f"{k}_dram", a.shape, mybir.dt.from_np(a.dtype), kind="ExternalInput").ap() for k, a in arrays.items()]
    y = nc.dram_tensor("y_dram", (B, 1), F32, kind="ExternalOutput").ap()
    x1_dram = nc.dram_tensor("x1_scratch", (O, 2 * N), F32, kind="Internal").ap()
    cin_kernel(nc, *args, x1_dram, y)
    result = run_bass_kernel_spmd(nc, [{f"{k}_dram": a for k, a in arrays.items()}], core_ids=[0])
    return result.results[0]["y_dram"]
```

```python
from contextlib import ExitStack

import numpy as np

import concourse.bass as bass
from concourse import mybir

F32 = mybir.dt.float32
F32R = mybir.dt.float32r
ALU = mybir.AluOpType
ACT = mybir.ActivationFunctionType
AX_X = mybir.AxisListType.X

B, F, D = 512, 39, 64
O = 64
SIDE_B = 8
N = SIDE_B * D
PAIRS = B // (2 * SIDE_B)

U1, V1 = 6, 20
J1, I1 = -(-F // V1), F // U1
EXTRA = F - U1 * I1
KX = EXTRA * F
GROUPS = ((0, 3), (3, 3))
GROUP = 4
U2, V2 = 8, 16
J2, I2 = -(-F // U2), O // V2
K1, K2 = U1 * V1, U2 * V2
REST = 64
MH = REST + F
KH = MH + 1
POOL_TILES = 2

UNITS1, UNITS2 = len(GROUPS) * J1, J2
ORDER = [(1, k) for k in range(UNITS1)] + [(2, k) for k in range(UNITS2)]
UNITS = len(ORDER)
SPREAD_SLOTS = [(j * len(GROUPS), (j + 1) * len(GROUPS) - 1) for j in range(J1)] + [(t, t) for t in range(UNITS1, UNITS)]
RING = 5
AHEAD = 2
T_X2 = 1
T_X1SUM = 2
T_H = (0, 3, 4, 5)
T_G = 7
T_X0 = 3
T_W3 = (1, 3)
T_LAST1 = UNITS1 - 1
T_EXTRA = 1
SEL1 = J1 * K1 + KX
SEL = SEL1 + J2 * K2
QUARTERS = 4
QB = SIDE_B // QUARTERS
X1_READS = U2
BUFS = 3
assert KX <= K1 and GROUPS[-1][1] < GROUP and UNITS % BUFS == 0 and UNITS1 + UNITS2 == UNITS


def tiles_of(layer, number):
    if layer == 2:
        return number, 0, I2
    j, group = divmod(number, len(GROUPS))
    return j, *GROUPS[group]


class Step:

    def __init__(self, n, static, trip=0):
        self.n, self.static, self.trip = n, static, trip
        self.has1 = static < PAIRS
        self.has2 = static >= 1
        self.has_h = 1 <= static < PAIRS - 1
        self.slots = [t for t, (layer, _) in enumerate(ORDER) if (layer == 1 and self.has1) or (layer == 2 and self.has2)]
        self.spreads = [w for w, (first, _) in enumerate(SPREAD_SLOTS) if first in self.slots]
        self.before = 0 if static == 0 else (n - 1) * UNITS + UNITS1
        self.spreads_before = 0 if static == 0 else (n - 1) * len(SPREAD_SLOTS) + J1

    def back(self):
        return Step(self.n - 1, self.static - 1, self.trip)

    def number(self, t):
        return self.before + self.slots.index(t)

    def product_buffer(self, t):
        return Step(self.static, self.static).number(t) % BUFS

    def spread_number(self, w):
        return self.spreads_before + self.spreads.index(w)

    def hpool_buffer(self, w):
        return Step(self.static, self.static).spread_number(w) % BUFS


def spread_of(t):
    return next(w for w, (first, last) in enumerate(SPREAD_SLOTS) if first <= t <= last)


def spread_ahead(step, following, t):
    k = step.slots.index(t) + AHEAD
    if k >= len(step.slots):
        if following is None:
            return None
        k, step = k - len(step.slots), following
    first = step.slots[k]
    w = spread_of(first)
    return (step, w) if SPREAD_SLOTS[w][0] == first else None


def last_user(step, w, side):
    wanted = (2 * w + side) % RING
    sides = [(step, v, s) for v in step.spreads for s in range(2) if (v, s) < (w, side)]
    if step.static:
        back = step.back()
        sides = [(back, v, s) for v in back.spreads for s in range(2)] + sides
    same = [(st, SPREAD_SLOTS[v][1], s) for st, v, s in sides if (2 * v + s) % RING == wanted]
    return same[-1] if same else None


def last_hpool_user(step, w):
    spreads = [(step, v) for v in step.spreads if v < w]
    if step.static:
        back = step.back()
        spreads = [(back, v) for v in back.spreads] + spreads
    return (spreads[-BUFS][0], SPREAD_SLOTS[spreads[-BUFS][1]][1]) if len(spreads) >= BUFS else None


def steps_of(eng, run, last=PAIRS):
    first = 2
    for n in range(first):
        run(Step(n, n), Step(n + 1, n + 1))
    trips = (PAIRS - 1 - first) // BUFS
    with eng.Fori(0, trips) as trip:
        for k in range(BUFS):
            n = first + k
            run(Step(trip * BUFS + n, n, trip), Step(trip * BUFS + n + 1, n + 1, trip))
    for n in range(first + trips * BUFS, last + 1):
        run(Step(n, n), Step(n + 1, n + 1) if n < PAIRS else None)


def wait(eng, sem, value):
    if not isinstance(value, int) or value > 0:
        eng.wait_ge(sem, value)


def cin_kernel(nc, x0t, x0h, x0e, gw, c1_in, c2_in, cw3, cols, rows, sel_in, x1_dram, out):
    with ExitStack() as ctx:
        def sb(name, shape, dt=F32):
            return ctx.enter_context(nc.sbuf_tensor(name, shape, dt))

        def sem(name):
            return ctx.enter_context(nc.semaphore(name))

        x0t_sb = sb("x0t_sb", [2 * D, BUFS, 2 * SIDE_B * F])
        x0split = sb("x0split", [2 * D, BUFS, SIDE_B, 2 * REST], F32R)
        x0rep = sb("x0rep", [128, BUFS, GROUP, 2 * N])
        gw_sb = sb("gw_sb", [2 * D, 3 * D])
        gwsplit = sb("gwsplit", [2 * D, 2, 3 * D], F32R)
        gb_sb = sb("gb_sb", [128, 3 * D])
        gbsplit = sb("gbsplit", [128, 3 * D], F32R)
        c1 = sb("c1", [K1, J1 * I1 + 1, O])
        c2 = sb("c2", [K2, J2, I2, O])
        w3 = sb("w3", [KH, 2 * O])
        w3t = sb("w3t", [O, F + 1])
        cols_sb = sb("cols_sb", [128, 8])
        rows_sb = sb("rows_sb", [2, 2 * O + 1])
        sel_raw = sb("sel_raw", [128, SEL + O])
        sel = sb("sel", [128, SEL], F32R)
        hsplit = sb("hsplit", [128, BUFS, 2, 2, N], F32R)
        h3 = sb("h3", [KH, BUFS, N])
        x1_sb = sb("x1_sb", [128, N])
        x1rep = sb("x1rep", [K2, I2, 2 * N])
        hpool = sb("hpool", [K2, BUFS, N])
        prod = sb("prod", [128, BUFS, 2, I2, N])
        g_sb = sb("g_sb", [128, N])
        x2g = sb("x2g", [128, N])
        x1sum = sb("x1sum", [128, PAIRS * SIDE_B])
        ysum = sb("ysum", [128, PAIRS * SIDE_B])
        const_row = sb("const_row", [2, O])
        const_y = sb("const_y", [2, 2])
        y_sb = sb("y_sb", [2, PAIRS * SIDE_B])

        ps = ctx.enter_context(nc.psum_tensor("ps", [128, 8, N], F32))
        ring, misc, acc1, acc2 = [ps[:, k, :] for k in range(RING)], ps[:, 5, :], ps[:, 6, :], ps[:, 7, :]

        cb1, cb2, fc2 = cols_sb[:, 0:1], cols_sb[:, 1:2], cols_sb[:, 2:3]
        fc1_sides, one_sides = cols_sb[:, 3:5], cols_sb[:, 5:7]
        sel1 = sel[:, 0:J1 * K1].rearrange("k (j p) -> k j p", j=J1)
        sel_extra = sel[:, J1 * K1:SEL1]
        sel2 = sel[:, SEL1:SEL].rearrange("k (j p) -> k j p", j=J2)
        fc3, ident = cols_sb[0:O, 7:8], sel_raw[0:O, SEL:SEL + O]

        gw_in = sem("gw_in")
        x0extra_in = sem("x0extra_in")
        gw_head = sem("gw_head")
        gw_rest = sem("gw_rest")
        x0_head = sem("x0_head")
        x0_rest = sem("x0_rest")
        sel_in_1 = sem("sel_in_1")
        sel_in_2 = sem("sel_in_2")
        c1_loaded = sem("c1_loaded")
        cols_in = sem("cols_in")
        c2_rows_in = sem("c2_rows_in")
        w3_in = sem("w3_in")
        x0t_in = [sem(f"x0t_in{k}") for k in range(BUFS)]
        x0rep_in = [sem(f"x0rep_in{k}") for k in range(BUFS)]
        zeros = sem("zeros")
        filled = sem("filled")
        sel_done = sem("sel_done")
        w3_flat = sem("w3_flat")
        w3_flat_copied = sem("w3_flat_copied")
        w3_turned = sem("w3_turned")
        w3_done = sem("w3_done")
        h_made = sem("h_made")
        h_head = sem("h_head")
        h_rest = sem("h_rest")
        spread = sem("spread")
        extra_spread = sem("extra_spread")
        hpool_copied = sem("hpool_copied")
        multiplied = sem("multiplied")
        pool_multiplied = sem("pool_multiplied")
        contracted = sem("contracted")
        x1_taken = sem("x1_taken")
        x1_stored = sem("x1_stored")
        x1_spread = sem("x1_spread")
        x1_summed = sem("x1_summed")
        g_made = sem("g_made")
        g_copied = sem("g_copied")
        x2_taken = sem("x2_taken")
        tables_loaded = sem("tables_loaded")
        const_steps = sem("const_steps")
        ysum_done = sem("ysum_done")
        y_made = sem("y_made")
        y_done = sem("y_done")
        y_out = sem("y_out")

        first_banks = (ring[0:4], (misc, acc1, ring[4], misc))
        w3_bank = ring[4]

        def acc1_of(step):
            return acc1 if step.static else acc2

        def acc2_of(step):
            return acc2 if step.static < PAIRS else acc1

        def fill(buf):
            for side in range(2):
                for layer in range(2):
                    bias = gbsplit[:, layer * D:(layer + 1) * D].bitcast(F32).unsqueeze(1).to_broadcast([128, SIDE_B, D])
                    nc.vector.tensor_copy(by_row(hsplit[:, buf, side, layer, :]), bias).then_inc(filled, 1)
            bias = gb_sb[0:KH, 2 * D:3 * D].unsqueeze(1).to_broadcast([KH, SIDE_B, D])
            nc.vector.tensor_copy(by_row(h3[:, buf, :]), bias).then_inc(filled, 1)

        def by_row(ap):
            return ap.rearrange("p (b e) -> p b e", e=D)

        def rest_x0(eng, m, buf):
            eng.wait_ge(x0_head, m + 1)
            engine = nc.vector if isinstance(m, int) and m == 0 else nc.gpsimd
            engine.tensor_tensor(out=x0_by_row(x0split[0:D, buf, :, :]),
                                 in0=x0t_sb[0:D, buf, :].rearrange("e (s b f) -> e s b f", s=2, f=F),
                                 in1=x0_by_row(x0split[0:D, buf, :, :].bitcast(F32)), op=ALU.subtract).then_inc(x0_rest, 1)

        def x0_by_row(ap):
            return ap.rearrange("e b (s f) -> e s b f", s=2)[:, :, :, 0:F]

        def extra_banks(step):
            return (acc2 if step.static else acc1), misc

        def group_buffer(static, group):
            return (len(GROUPS) * static + group) % BUFS

        def x0_tiles(eng, step, number, extra=False):
            j, group = divmod(number, len(GROUPS))
            if j == 0:
                loads = step.trip * len(GROUPS) + (len(GROUPS) * step.static + group) // BUFS + 1
                eng.wait_ge(x0rep_in[group_buffer(step.static, group)], loads * (16 * U1))
                if group == len(GROUPS) - 1 and extra:
                    eng.wait_ge(x0extra_in, (step.n + 1) * (16 * EXTRA))
            return x0rep[0:K1, group_buffer(step.static, group), 0:GROUPS[group][1], :]

        def x1_buffer(step):
            return x1rep[:, :, :] if step.static < PAIRS else x0rep[:, group_buffer(PAIRS, 0), :, :]

        def x1_tiles(eng, step, number):
            if number == 0:
                eng.wait_ge(x1_spread, step.n * (16 * X1_READS))
            return x1_buffer(step)

        block = ctx.enter_context(nc.Block())

        @block.sync
        def _(sp):
            def load_x0t(m, buf):
                for half in range(2):
                    sp.dma_start(x0t_sb[half * D:(half + 1) * D, buf, :],
                                 x0t[:, bass.ds(m * (2 * SIDE_B * F), 2 * SIDE_B * F)]).then_inc(x0t_in[buf], 16)

            def load_group(m, static, group):
                i0, tiles = GROUPS[group]
                buf = group_buffer(static, group)
                for u in range(U1):
                    row = x0h[u:u + 1, bass.ds(m * (I1 * 2 * N) + i0 * (2 * N), tiles * (2 * N))]
                    sp.dma_start(x0rep[u * V1:(u + 1) * V1, buf, 0:tiles, :].rearrange("p i n -> p (i n)"),
                                 row.to_broadcast([V1, tiles * 2 * N])).then_inc(x0rep_in[buf], 16)
                if group == len(GROUPS) - 1:
                    for u in range(EXTRA):
                        row = x0e[u:u + 1, bass.ds(m * (2 * N), 2 * N)]
                        sp.dma_start(x0rep[u * F:(u + 1) * F, buf, GROUP - 1, :], row.to_broadcast([F, 2 * N])).then_inc(x0extra_in, 16)

            def after_unit(step, t):
                sp.wait_ge(multiplied, 2 * (step.number(t) + 1))
                sp.wait_ge(pool_multiplied, step.number(t) + 1)

            def run(step, following):
                n, static = step.n, step.static
                reads_before, stores = n * (16 * X1_READS), (n + 1) * 32
                if not isinstance(n, int):
                    sp.compute_val(reads_before)
                    sp.compute_val(stores)
                if static + 2 < PAIRS:
                    wait(sp, x0_rest, n)
                    load_x0t(n + 2, (static + 2) % BUFS)
                if static + 1 < PAIRS:
                    after_unit(step, T_LAST1 - 1)
                    load_group(n + 1, static + 1, 1)
                if static + 2 < PAIRS:
                    after_unit(step, T_LAST1)
                    load_group(n + 2, static + 2, 0)
                sp.wait_ge(x1_taken, n + 1)
                wait(sp, x1_spread, reads_before)
                for side in range(2):
                    sp.dma_start(x1_dram[:, side * N:(side + 1) * N], x1_sb[side * O:(side + 1) * O, :]).then_inc(x1_stored, 16)
                if static == 0:
                    sp.wait_ge(w3_flat, 1)
                elif static < PAIRS - 1:
                    after_unit(step, UNITS - 1)
                else:
                    after_unit(step.back(), T_LAST1)
                sp.wait_ge(x1_stored, stores)
                by_m = x1_dram.rearrange("(i v) n -> v i n", v=V2)
                for u in range(X1_READS):
                    sp.dma_start(x1_buffer(following)[u * V2:(u + 1) * V2, :, :], by_m).then_inc(x1_spread, 16)

            for half in range(2):
                sp.dma_start(gw_sb[half * D:(half + 1) * D, :], gw[0:D, :]).then_inc(gw_in, 16)
            load_x0t(0, 0)
            sp.dma_start(gb_sb[:, :], gw[D:D + 1, :].to_broadcast([128, 3 * D])).then_inc(gw_in, 16)
            load_x0t(1, 1)
            first = SEL1
            sp.dma_start(sel_raw[:, 0:first], sel_in[:, 0:first]).then_inc(sel_in_1, 16)
            load_group(0, 0, 0)
            sp.dma_start(c1[:, :, :].rearrange("p i o -> p (i o)"), c1_in[:, :]).then_inc(c1_loaded, 16)
            sp.dma_start(cols_sb[:, :], cols[:, :]).then_inc(cols_in, 16)
            load_group(0, 0, 1)
            sp.dma_start(x1rep[0:O, :, :].rearrange("p i n -> p (i n)")[:, 0:F * O], cw3[:, :]).then_inc(w3_in, 16)
            sp.dma_start(sel_raw[:, first:], sel_in[:, first:]).then_inc(sel_in_2, 16)
            load_group(1, 1, 0)
            sp.dma_start(c2[:, :, :, :].rearrange("p j i o -> p (j i o)"), c2_in[:, :]).then_inc(c2_rows_in, 16)
            sp.dma_start(rows_sb[:, :], rows[:, :]).then_inc(c2_rows_in, 16)
            steps_of(sp, run, PAIRS - 1)
            sp.wait_ge(y_done, 1)
            sp.dma_start(out.rearrange("(n s b) o -> s n (b o)", s=2, b=SIDE_B),
                         y_sb[:, :].rearrange("s (n b) -> s n b", b=SIDE_B)).then_inc(y_out, 16)
            sp.wait_ge(y_out, 16)

        @block.tensor
        def _(pe):
            def make_h(q, bank, m, buf):
                if q == 0:
                    pe.wait_ge(x0_rest, m + 1)
                for b in range(QB):
                    for part in range(2):
                        last = nc.tensor.matmul(bank[0:MH, b * 3 * D:(b + 1) * 3 * D], x0split[:, buf, q * QB + b, 0:MH],
                                                gwsplit[:, part, :], start=(part == 0), stop=(part == 1))
                last.then_inc(h_made, 1)

            def spread_h(step, w):
                first, _ = SPREAD_SLOTS[w]
                layer, number = ORDER[first]
                pair_static = step.static if layer == 1 else step.static - 1
                if first == 0:
                    pe.wait_ge(h_rest, (step.n + 1) * QUARTERS)
                if step.static == 1 and layer == 2 and number == 0:
                    pe.wait_ge(w3_done, 1)
                j, k = tiles_of(layer, number)[0], (K1, K2)[layer - 1]
                lhs = (sel1, sel2)[layer - 1][0:KH, j, :]
                for side in range(2):
                    user = last_user(step, w, side)
                    if user:
                        user_step, user_slot, user_side = user
                        pe.wait_ge(multiplied, 2 * user_step.number(user_slot) + user_side + 1)
                    nc.tensor.matmul(ring[(2 * w + side) % RING][0:k, :], lhs, hsplit[0:KH, pair_static % BUFS, side, layer - 1, :],
                                     start=True, stop=True).then_inc(spread, 1)

            def spread_extra(step):
                n = step.n
                for side, bank in enumerate(extra_banks(step)):
                    if side == 0:
                        if step.static >= 2:
                            pe.wait_ge(x2_taken, n - 1)
                        elif step.static == 1:
                            pe.wait_ge(x1_taken, 1)
                        else:
                            pe.wait_ge(h_rest, QUARTERS + 2)
                    elif step.static == 0:
                        pe.wait_ge(h_rest, 2 * QUARTERS)
                    elif step.has_h:
                        pe.wait_ge(h_rest, (n + 1) * QUARTERS + 1)
                    else:
                        pe.wait_ge(g_copied, n - 1)
                    nc.tensor.matmul(bank[0:KX, :], sel_extra[0:KH, :], hsplit[0:KH, step.static % BUFS, side, 0, :],
                                     start=True, stop=True).then_inc(extra_spread, 1)

            def contract(step, t):
                layer, number = ORDER[t]
                j, i0, tiles = tiles_of(layer, number)
                acc, k, units = (acc1_of(step), K1, UNITS1) if layer == 1 else (acc2_of(step), K2, UNITS2)
                if number == 0:
                    if layer == 1:
                        wait(pe, x1_taken, step.n if step.static >= 2 else 0)
                    elif step.static == 1:
                        pe.wait_ge(x1_taken, 1)
                    elif step.static < PAIRS:
                        pe.wait_ge(x2_taken, step.n - 1)
                    else:
                        pe.wait_ge(x1_taken, PAIRS)
                pe.wait_ge(multiplied, 2 * (step.number(t) + 1))
                parts = [(i, k, c1[0:k, j * I1 + i0 + i, :] if layer == 1 else c2[:, j, i, :]) for i in range(tiles)]
                if t == T_LAST1:
                    parts.append((GROUP - 1, KX, c1[0:KX, J1 * I1, :]))
                for i, rows_, weights in parts:
                    if i == tiles - POOL_TILES:
                        pe.wait_ge(pool_multiplied, step.number(t) + 1)
                    for side in range(2):
                        last = nc.tensor.matmul(acc[side * O:(side + 1) * O, :], weights,
                                                prod[0:rows_, step.product_buffer(t), side, i, :],
                                                start=(number == 0 and i == 0), stop=(number == units - 1 and i == parts[-1][0]))
                last.then_inc(contracted, 1)

            def make_w3(t):
                if t == T_W3[0]:
                    pe.wait_ge(w3_in, 16)
                    pe.wait_ge(cols_in, 16)
                    cw3_rows = x1rep[0:O, :, :].rearrange("p i n -> p (i n)")
                    pe.wait_ge(h_rest, QUARTERS + 3)
                    for h in range(F):
                        last = nc.tensor.matmul(w3_bank[0:O, h:h + 1], cw3_rows[:, h * O:(h + 1) * O], fc3, start=True, stop=True)
                    last.then_inc(w3_flat, 1)
                elif t == T_W3[1]:
                    pe.wait_ge(w3_flat_copied, 1)
                    pe.wait_ge(sel_in_2, 16)
                    pe.wait_ge(sel_done, 2)
                    pe.wait_ge(c2_rows_in, 32)
                    for side in range(2):
                        last = nc.tensor.matmul(w3_bank[side * REST:side * REST + F + 1, O:2 * O], w3t[:, :], ident, start=True, stop=True)
                    last.then_inc(w3_turned, 1)

            def run(step, following):
                n = step.n
                for t in step.slots:
                    if t == (T_EXTRA if step.static else T_EXTRA + 1) and step.has1:
                        spread_extra(step)
                    found = spread_ahead(step, following, t)
                    if found:
                        spread_h(*found)
                    if t == T_G and step.has2:
                        if step.has_h:
                            pe.wait_ge(h_rest, (n + 2) * QUARTERS)
                        else:
                            pe.wait_ge(g_copied, n - 1)
                        nc.tensor.matmul(misc, w3[:, :], h3[0:KH, (step.static - 1) % BUFS, :],
                                         start=True, stop=True).then_inc(g_made, 1)
                    if t in T_H and step.has_h:
                        q = T_H.index(t)
                        if q == 0:
                            wait(pe, g_copied, n - 1)
                        elif q == 1:
                            pe.wait_ge(multiplied, 2 * (step.number(T_LAST1) + 1))
                        else:
                            pe.wait_ge(h_rest, (n + 1) * QUARTERS + q)
                        make_h(q, misc, n + 1, (step.static + 1) % BUFS)
                    contract(step, t)
                    if step.static == 0:
                        if t == 0:
                            pe.wait_ge(h_rest, QUARTERS + 1)
                            make_h(QUARTERS - 1, first_banks[1][-1], 1, 1)
                        make_w3(t)

            pe.wait_ge(zeros, 2)
            pe.wait_ge(gw_rest, 1)
            for q in range(QUARTERS):
                make_h(q, first_banks[0][q], 0, 0)

            make_h(0, first_banks[1][0], 1, 1)
            pe.wait_ge(sel_done, 1)
            spread_h(Step(0, 0), 0)
            for q in range(1, QUARTERS - 1):
                make_h(q, first_banks[1][q], 1, 1)
            pe.wait_ge(c1_loaded, 16)
            steps_of(pe, run)
            pe.wait_ge(g_copied, PAIRS)
            pe.wait_ge(x1_summed, PAIRS)
            nc.tensor.matmul(misc[0:2, 0:PAIRS * SIDE_B], fc1_sides, x1sum[:, :], start=True, stop=False)
            pe.wait_ge(ysum_done, PAIRS)
            nc.tensor.matmul(misc[0:2, 0:PAIRS * SIDE_B], one_sides, ysum[:, :], start=False, stop=True).then_inc(y_made, 1)

        @block.scalar
        def _(act):
            def heads(q, bank, m, buf):
                act.wait_ge(h_made, m * QUARTERS + q + 1)
                cut = slice(q * QB * D, (q + 1) * QB * D)
                for side in range(2):
                    rows_ = slice(side * REST, side * REST + F)
                    src = bank[rows_, 0:QB * 3 * D].rearrange("h (b l e) -> h b l e", b=QB, l=3)
                    dst = hsplit[rows_, buf, side, :, cut].rearrange("h l (b e) -> h b l e", b=QB)
                    nc.scalar.copy(dst, src[:, :, 0:2, :])
                    last = nc.scalar.copy(h3[rows_, buf, cut].rearrange("h (b e) -> h b e", b=QB), src[:, :, 2, :])
                last.then_inc(h_head, 1)

            def head_x0(m, static, trip):
                buf = static % BUFS
                act.wait_ge(x0t_in[buf], (trip + static // BUFS + 1) * 32)
                wait(act, h_made, (m - BUFS + 1) * QUARTERS if static >= BUFS else 0)
                nc.scalar.copy(x0_by_row(x0split[:, buf, :, :]), x0t_sb[:, buf, :].rearrange("e (s b f) -> e s b f", s=2, f=F)).then_inc(x0_head, 1)

            def copy_for_pool(step, w):
                k = (K1, K2)[ORDER[SPREAD_SLOTS[w][0]][0] - 1]
                act.wait_ge(spread, 2 * (step.spread_number(w) + 1))
                user = last_hpool_user(step, w)
                if user:
                    user_step, user_slot = user
                    act.wait_ge(pool_multiplied, user_step.number(user_slot) + 1)
                nc.scalar.copy(hpool[0:k, step.hpool_buffer(w), :], ring[(2 * w + 1) % RING][0:k, :]).then_inc(hpool_copied, 1)

            def run(step, following):
                n = step.n
                for t in step.slots:
                    found = spread_ahead(step, following, t)
                    if found:
                        copy_for_pool(*found)
                    if t == T_G and step.has2:
                        act.wait_ge(g_made, n)
                        wait(act, x2_taken, n - 1)
                        nc.scalar.activation(g_sb[:, :], misc, ACT.Identity, bias=fc2).then_inc(g_copied, 1)
                    if t == T_X0 and step.static + 2 < PAIRS:
                        head_x0(n + 2, step.static + 2, step.trip)
                    if t in T_H and step.has_h:
                        if step.static == 1 and t == T_H[0]:
                            act.wait_ge(filled, 15)
                        heads(T_H.index(t), misc, n + 1, (step.static + 1) % BUFS)
                    if t == 0 and step.static == 0:
                        heads(QUARTERS - 1, first_banks[1][-1], 1, 1)
                    if t == T_LAST1:
                        act.wait_ge(contracted, step.number(T_LAST1) + 1)
                        wait(act, x1_stored, n * 32)
                        wait(act, x1_summed, n)
                        nc.scalar.activation(x1_sb[:, :], acc1_of(step), ACT.Identity, bias=cb1).then_inc(x1_taken, 1)

            act.wait_ge(zeros, 1)
            nc.scalar.copy(x2g[0:1, 0:1], w3[0:1, 0:1]).then_inc(tables_loaded, 1)
            act.wait_ge(gw_in, 48)
            nc.scalar.copy(gwsplit[:, 0, :], gw_sb[:, :]).then_inc(gw_head, 1)
            head_x0(0, 0, 0)
            nc.scalar.copy(gbsplit[:, :], gb_sb[:, :]).then_inc(gw_head, 1)
            head_x0(1, 1, 0)
            act.wait_ge(filled, 5)
            for q in range(QUARTERS):
                heads(q, first_banks[0][q], 0, 0)
            copy_for_pool(Step(0, 0), 0)
            act.wait_ge(filled, 10)
            for q in range(QUARTERS - 1):
                heads(q, first_banks[1][q], 1, 1)
            act.wait_ge(cols_in, 16)
            steps_of(act, run)

        @block.vector
        def _(dve):
            def rests(q, bank, m, buf):
                dve.wait_ge(h_head, m * QUARTERS + q + 1)
                cut = slice(q * QB * D, (q + 1) * QB * D)
                for side in range(2):
                    here, there = slice(side * REST, side * REST + F), slice((1 - side) * REST, (1 - side) * REST + F)
                    src = bank[here, 0:QB * 3 * D].rearrange("h (b l e) -> h b l e", b=QB, l=3)
                    head = hsplit[here, buf, side, :, cut].bitcast(F32).rearrange("h l (b e) -> h b l e", b=QB)
                    rest = hsplit[there, buf, side, :, cut].rearrange("h l (b e) -> h b l e", b=QB)
                    last = nc.vector.tensor_tensor(out=rest, in0=src[:, :, 0:2, :], in1=head, op=ALU.subtract)
                last.then_inc(h_rest, 1)

            def multiply(step, t):
                layer, number = ORDER[t]
                j, i0, tiles = tiles_of(layer, number)
                k, w = (K1, K2)[layer - 1], spread_of(t)
                if layer == 1:
                    x = x0_tiles(dve, step, number, extra=True)
                else:
                    x = x1_tiles(dve, step, number)
                wait(dve, contracted, step.number(t) - BUFS + 1)
                for side in range(2):
                    own = tiles - side * POOL_TILES
                    if t == SPREAD_SLOTS[w][0]:
                        dve.wait_ge(spread, 2 * step.spread_number(w) + side + 1)
                        if side == 1:
                            dve.wait_ge(hpool_copied, step.spread_number(w) + 1)
                    h = ring[(2 * w + side) % RING][0:k, :].unsqueeze(1).to_broadcast([k, own, N])
                    last = nc.vector.tensor_tensor(out=prod[0:k, step.product_buffer(t), side, 0:own, :], in0=h,
                                                   in1=x[:, 0:own, side * N:(side + 1) * N], op=ALU.mult)
                    if t == T_LAST1:
                        dve.wait_ge(extra_spread, 2 * step.n + side + 1)
                        buf = group_buffer(step.static, len(GROUPS) - 1)
                        last = nc.vector.tensor_tensor(out=prod[0:KX, step.product_buffer(t), side, GROUP - 1, :],
                                                       in0=extra_banks(step)[side][0:KX, :],
                                                       in1=x0rep[0:KX, buf, GROUP - 1, side * N:(side + 1) * N], op=ALU.mult)
                    last.then_inc(multiplied, 1)

            def sum_x1(m):
                dve.wait_ge(x1_taken, m + 1)
                nc.vector.tensor_reduce(x1sum[:, bass.ds(m * SIDE_B, SIDE_B)], by_row(x1_sb[:, :]), AX_X, ALU.add).then_inc(x1_summed, 1)

            def take_x2(m, acc, end_of_units):
                dve.wait_ge(contracted, end_of_units)
                dve.wait_ge(g_copied, m + 1)
                nc.vector.scalar_tensor_tensor(out=x2g[:, :], in0=acc[:, :], scalar=cb2, in1=g_sb[:, :],
                                               op0=ALU.add, op1=ALU.mult).then_inc(x2_taken, 1)
                dve.wait_ge(x2_taken, m + 1)
                nc.vector.tensor_reduce(ysum[:, bass.ds(m * SIDE_B, SIDE_B)], by_row(x2g[:, :]), AX_X, ALU.add).then_inc(ysum_done, 1)

            def first_extras(t):
                if t == 0:
                    dve.wait_ge(filled, 10)
                    rests(0, first_banks[1][0], 1, 1)
                    rests(1, first_banks[1][1], 1, 1)
                if t == 1:
                    for q in range(2, QUARTERS):
                        rests(q, first_banks[1][q], 1, 1)
                    dve.wait_ge(sel_in_2, 16)
                    nc.vector.tensor_copy(sel[:, SEL1:], sel_raw[:, SEL1:SEL]).then_inc(sel_done, 1)
                    fill(2)
                if t == T_W3[1]:
                    dve.wait_ge(w3_flat, 1)
                    nc.vector.tensor_copy(w3t[:, 0:F], w3_bank[0:O, 0:F])
                    nc.vector.tensor_reduce(w3t[:, F:F + 1], w3_bank[0:O, 0:F], AX_X, ALU.add).then_inc(w3_flat_copied, 1)
                if t == T_LAST1:
                    dve.wait_ge(cols_in, 16)
                    dve.wait_ge(c2_rows_in, 32)
                    nc.vector.tensor_tensor(out=const_row[:, :], in0=rows_sb[:, 0:O], in1=rows_sb[:, O:2 * O], op=ALU.mult).then_inc(const_steps, 1)
                    dve.wait_ge(const_steps, 1)
                    nc.vector.tensor_reduce(const_y[:, 0:1], const_row[:, :], AX_X, ALU.add).then_inc(const_steps, 1)
                    dve.wait_ge(const_steps, 2)
                    nc.vector.tensor_scalar(const_y[:, 1:2], const_y[:, 0:1], float(D), rows_sb[:, 2 * O:2 * O + 1],
                                            ALU.mult, ALU.add).then_inc(const_steps, 1)

            def run(step, following):
                late = 0 if step.has1 else UNITS1
                for t in step.slots:
                    multiply(step, t)
                    if step.static == 0:
                        first_extras(t)
                    if step.static == 1 and t == 1:
                        dve.wait_ge(w3_turned, 1)
                        for side in range(2):
                            rows_ = slice(side * REST, side * REST + F + 1)
                            last = nc.vector.tensor_copy(w3[rows_, side * O:(side + 1) * O], w3_bank[rows_, O:2 * O])
                        last.then_inc(w3_done, 1)
                    if t == T_X2 + late and step.static >= 2:
                        take_x2(step.n - 2, acc2, step.before)
                    if t == T_X1SUM + late and step.has2:
                        sum_x1(step.n - 1)
                    if t - 1 in T_H and step.has_h:
                        rests(T_H.index(t - 1), misc, step.n + 1, (step.static + 1) % BUFS)

            nc.vector.memset(w3[:, :], 0.0).then_inc(zeros, 1)
            nc.vector.memset(x0split[:, :, :, F:REST].rearrange("p k b n -> p (k b) n").bitcast(F32), 0.0).then_inc(zeros, 1)
            dve.wait_ge(gw_head, 1)
            nc.vector.tensor_tensor(out=gwsplit[:, 1, :], in0=gw_sb[:, :], in1=gwsplit[:, 0, :].bitcast(F32), op=ALU.subtract).then_inc(gw_rest, 1)
            rest_x0(dve, 0, 0)
            dve.wait_ge(gw_head, 2)
            nc.vector.tensor_tensor(out=gbsplit[REST:2 * REST, :], in0=gb_sb[REST:2 * REST, :],
                                    in1=gbsplit[REST:2 * REST, :].bitcast(F32), op=ALU.subtract).then_inc(gw_rest, 1)
            dve.wait_ge(gw_rest, 2)
            fill(0)
            dve.wait_ge(filled, 5)
            dve.wait_ge(sel_in_1, 16)
            nc.vector.tensor_copy(sel[:, 0:SEL1], sel_raw[:, 0:SEL1]).then_inc(sel_done, 1)
            for q in range(QUARTERS):
                rests(q, first_banks[0][q], 0, 0)
            fill(1)
            steps_of(dve, run)
            last_step = Step(PAIRS, PAIRS)
            take_x2(PAIRS - 1, acc2_of(last_step), last_step.before + UNITS2)
            dve.wait_ge(const_steps, 3)
            dve.wait_ge(y_made, 1)
            nc.vector.tensor_scalar(y_sb[:, :], misc[0:2, 0:PAIRS * SIDE_B], const_y[:, 1:2], None, ALU.add).then_inc(y_done, 1)

        @block.gpsimd
        def _(pool):
            def run(step, following):
                for t in step.slots:
                    layer, number = ORDER[t]
                    j, i0, tiles = tiles_of(layer, number)
                    k, w = (K1, K2)[layer - 1], spread_of(t)
                    if layer == 1:
                        x = x0_tiles(pool, step, number)
                    else:
                        x = x1_tiles(pool, step, number)
                    wait(pool, contracted, step.number(t) - BUFS + 1)
                    if t == SPREAD_SLOTS[w][0]:
                        pool.wait_ge(hpool_copied, step.spread_number(w) + 1)
                    h = hpool[0:k, step.hpool_buffer(w), :].unsqueeze(1).to_broadcast([k, POOL_TILES, N])
                    own = slice(tiles - POOL_TILES, tiles)
                    nc.gpsimd.tensor_tensor(out=prod[0:k, step.product_buffer(t), 1, own, :], in0=h,
                                            in1=x[:, own, N:2 * N], op=ALU.mult).then_inc(pool_multiplied, 1)
                    if t == T_X0 + (1 if step.static else 0) and step.static + 2 < PAIRS:
                        rest_x0(pool, step.n + 2, (step.static + 2) % BUFS)

            pool.wait_ge(x0_rest, 1)
            rest_x0(pool, 1, 1)
            steps_of(pool, run)


def kernel(**inputs):
    import concourse.bacc as bacc
    from concourse.bass_utils import run_bass_kernel_spmd

    p = {k: np.asarray(v) for k, v in inputs.items()}
    x0, fc = p["r_feature_emb"], p["L0_rec_fcW"]
    gw = np.concatenate([np.concatenate([p[f"L0_rec_gw{l}"], p[f"L0_rec_gb{l}"][None]], 0) for l in (1, 2, 3)], 1)
    w = p["L0_rec_cw1"].transpose(1, 2, 0)
    c1 = np.zeros((K1, J1 * I1 + 1, O), np.float32)
    main = np.zeros((J1 * V1, I1 * U1, O), np.float32)
    main[:F] = w[:, :I1 * U1]
    c1[:, :J1 * I1] = main.reshape(J1, V1, I1, U1, O).transpose(3, 1, 0, 2, 4).reshape(K1, -1, O)
    c1[:KX, J1 * I1] = w[:, I1 * U1:].transpose(1, 0, 2).reshape(KX, O)
    c1 = c1.reshape(K1, -1)
    x0m = x0.transpose(1, 0, 2).reshape(F, -1)
    x0h = x0m[:I1 * U1].reshape(I1, U1, PAIRS, 2 * N).transpose(1, 2, 0, 3).reshape(U1, -1)
    x0e = x0m[I1 * U1:]
    c2 = np.zeros((J2 * U2, I2, V2, O), np.float32)
    c2[:F] = p["L0_rec_cw2"].transpose(1, 2, 0).reshape(F, I2, V2, O)
    c2 = c2.reshape(J2, U2, I2, V2, O).transpose(1, 3, 0, 2, 4).reshape(K2, -1)
    cols = np.zeros((128, 8), np.float32)
    cols[:O, 7] = fc[0, 2 * O:]
    for side in range(2):
        half = slice(side * O, (side + 1) * O)
        cols[half, 0], cols[half, 1], cols[half, 2] = p["L0_rec_cb1"], p["L0_rec_cb2"], fc[0, O:2 * O]
        cols[half, 3 + side], cols[half, 5 + side] = fc[0, :O], 1.0
    rows = np.stack([np.concatenate([fc[0, 2 * O:], p["L0_rec_cb3"], p["L0_rec_fcb"]])] * 2)
    sel1, sel2 = (np.zeros((128, n, k), np.float32) for n, k in ((J1, K1), (J2, K2)))
    for h in range(F):
        for row in (h, REST + h, F, MH):
            sel1[row, h // V1, h % V1::V1] = 1.0
            sel2[row, h // U2, (h % U2) * V2:(h % U2 + 1) * V2] = 1.0
    sel_extra = np.zeros((128, EXTRA, F), np.float32)
    sel_extra[np.arange(F), :, np.arange(F)] = sel_extra[REST + np.arange(F), :, np.arange(F)] = 1.0
    sel_extra[F] = sel_extra[MH] = 1.0
    sel = np.concatenate([a.reshape(128, -1) for a in (sel1, sel_extra, sel2)] + [np.eye(128, O, dtype=np.float32)], 1)
    x0t = x0.transpose(2, 0, 1).reshape(D, -1)
    arrays = {
        "x0t": x0t, "x0h": x0h, "x0e": x0e, "gw": gw, "c1": c1,
        "c2": c2, "cw3": p["L0_rec_cw3"].reshape(O, -1), "cols": cols, "rows": rows, "sel": sel,
    }
    arrays = {k: np.ascontiguousarray(v) for k, v in arrays.items()}
    nc = bacc.Bacc("TRN2", target_bir_lowering=False, num_devices=1)
    args = [nc.dram_tensor(f"{k}_dram", a.shape, mybir.dt.from_np(a.dtype), kind="ExternalInput").ap() for k, a in arrays.items()]
    y = nc.dram_tensor("y_dram", (B, 1), F32, kind="ExternalOutput").ap()
    x1_dram = nc.dram_tensor("x1_scratch", (O, 2 * N), F32, kind="Internal").ap()
    cin_kernel(nc, *args, x1_dram, y)
    result = run_bass_kernel_spmd(nc, [{f"{k}_dram": a for k, a in arrays.items()}], core_ids=[0])
    return result.results[0]["y_dram"]
```
